# Optimizing a Trainium2 kernel written in Bass

```python
import numpy as np
import jax
import jax.numpy as jnp

def _softmax(x, axis=-1):
    return jax.nn.softmax(x, axis=axis)

def _gelu(x):
    return jax.nn.gelu(x, approximate=True)

def _silu(x):
    return jax.nn.silu(x)

def _sigmoid(x):
    return jax.nn.sigmoid(x)

def _layernorm(x, axis=-1, eps=1e-05):
    m = jnp.mean(x, axis=axis, keepdims=True)
    v = jnp.var(x, axis=axis, keepdims=True)
    return (x - m) / jnp.sqrt(v + eps)

def _scatter_add(tgt, idx, src, axis=0):
    return tgt.at[idx].add(src)

def _segment_sum(src, seg, n):
    return jax.ops.segment_sum(src, seg, n)
kernel_name = 'mk_xattn_ffn_d4_seqx_r8_f6fcfd'

def setup_inputs(seed: int=0):
    np.random.seed(seed)
    _w = jnp.asarray

    def _rec_inputs():
        import jax
        import jax.numpy as jnp
        _rk = jax.random.key(seed)
        x = -0.0002928 + 1 * jax.random.normal(jax.random.fold_in(_rk, 1), (64, 64, 128), jnp.float32)
        _lenS = 64 - jax.random.randint(jax.random.fold_in(_rk, 7), (64,), 0, max(1, 64 // 4) + 1, jnp.int32)
        _lenS2 = 64 - jax.random.randint(jax.random.fold_in(_rk, 8), (64,), 0, max(1, 64 // 4) + 1, jnp.int32)
        _ctx_1024P = jax.random.normal(jax.random.fold_in(_rk, 11), (64, 16, 128), jnp.float32)
        _ctx_1024c = jax.random.dirichlet(jax.random.fold_in(_rk, 511), 0.3 * jnp.ones((16,), jnp.float32), (64, 64))
        _ctx_1024t = jnp.einsum('bsk,bkd->bsd', _ctx_1024c, _ctx_1024P)
        _ctx_1024t = _ctx_1024t * jax.lax.rsqrt(jnp.mean(jnp.square(_ctx_1024t)) + 1e-12) * 0.953939
        ctx_1024 = -1.39393e-06 + 0.999914 * (_ctx_1024t + 0.3 * jax.random.normal(jax.random.fold_in(_rk, 611), (64, 64, 128), jnp.float32))
        _validS = jnp.arange(64)[None, :] < _lenS[:, None]
        _validS2 = jnp.arange(64)[None, :] < _lenS2[:, None]
        _causal = jnp.tril(jnp.ones((64, 64), dtype=bool))
        mask_BxS2_fk1 = jnp.where(jnp.broadcast_to(_validS2[:, :], (64, 64)), 1.0, 0.0).astype(jnp.float32)
        mask_BxS2_ik0 = jnp.where(jnp.broadcast_to(_validS2[:, :], (64, 64)), 0, 1).astype(jnp.int32)
        return (x, ctx_1024, mask_BxS2_fk1, mask_BxS2_ik0)
    x, ctx_1024, mask_BxS2_fk1, mask_BxS2_ik0 = _rec_inputs()

    def _L0_xattn_setup():
        import jax, jax.numpy as jnp
        import numpy as np
        B, S, D = (2, 256, 128)
        H, HD = (16, 64)
        key = jax.random.key(seed)
        ks = jax.random.split(key, 10)
        inp = {'queries': jax.random.normal(ks[0], (B, S, D), jnp.float32), 'keys': jax.random.normal(ks[1], (B, S, D), jnp.float32), 'values': jax.random.normal(ks[2], (B, S, D), jnp.float32), 'ind_q': (jax.random.uniform(ks[3], (B, S)) > 0.2).astype(jnp.float32), 'ind_k': (jax.random.uniform(ks[4], (B, S)) > 0.2).astype(jnp.float32), 'ind_v': (jax.random.uniform(ks[5], (B, S)) > 0.2).astype(jnp.float32), 'Wq': jax.random.normal(ks[6], (D, H * HD), jnp.float32) / np.sqrt(D), 'Wk': jax.random.normal(ks[7], (D, H * HD), jnp.float32) / np.sqrt(D), 'Wv': jax.random.normal(ks[8], (D, H * HD), jnp.float32) / np.sqrt(D), 'Wo': jax.random.normal(ks[9], (H * HD, D), jnp.float32) / np.sqrt(H * HD)}
        return inp
    _L0_xattn_all = _L0_xattn_setup()
    _L0_xattn_in = {k: v for k, v in _L0_xattn_all.items() if k in ('Wq', 'Wk', 'Wv', 'Wo')}
    del _L0_xattn_all

    def _L0_ffn_setup():
        import jax, jax.numpy as jnp
        import numpy as np
        N_EMBD = 128
        N_EXPERTS = 8
        TOP_K = 2
        CAPACITY_FACTOR = 1.25
        key = jax.random.key(seed)
        ks = jax.random.split(key, 8)
        B, T, C, E, H = (8, 256, N_EMBD, N_EXPERTS, 4 * N_EMBD)
        w = lambda k, shape: jax.random.normal(k, shape, jnp.float32) * 0.02
        return {'x': jax.random.normal(ks[0], (B, T, C), jnp.float32), 'rW1': w(ks[1], (C, H)), 'rb1': jnp.zeros((H,), jnp.float32), 'rW2': w(ks[2], (H, H)), 'rb2': jnp.zeros((H,), jnp.float32), 'rW3': w(ks[3], (H, E)), 'rb3': jnp.zeros((E,), jnp.float32), 'eW1': w(ks[4], (E, C, H)), 'eb1': jnp.zeros((E, H), jnp.float32), 'eW2': w(ks[5], (E, H, C)), 'eb2': jnp.zeros((E, C), jnp.float32)}
    _L0_ffn_all = _L0_ffn_setup()
    _L0_ffn_in = {k: v for k, v in _L0_ffn_all.items() if k in ('rW1', 'rb1', 'rW2', 'rb2', 'rW3', 'rb3', 'eW1', 'eb1', 'eW2', 'eb2')}
    del _L0_ffn_all

    def _L1_xattn_setup():
        import jax, jax.numpy as jnp
        import numpy as np
        B, LQ, LK, D = (4, 256, 256, 128)
        H = 16
        HD = D // H

        def _split_heads(x):
            b, l, _ = x.shape
            return x.reshape(b, l, H, HD).transpose(0, 2, 1, 3)
        key = jax.random.key(seed)
        ks = jax.random.split(key, 10)
        s = 0.02
        return {'hidden_states': jax.random.normal(ks[0], (B, LQ, D), jnp.float32), 'context': jax.random.normal(ks[1], (B, LK, D), jnp.float32), 'attention_mask': jax.random.randint(ks[2], (B, LK), 0, 2, jnp.int32), 'q_w': jax.random.normal(ks[3], (D, D), jnp.float32) * s, 'q_b': jnp.zeros((D,), jnp.float32), 'k_w': jax.random.normal(ks[4], (D, D), jnp.float32) * s, 'k_b': jnp.zeros((D,), jnp.float32), 'v_w': jax.random.normal(ks[5], (D, D), jnp.float32) * s, 'v_b': jnp.zeros((D,), jnp.float32)}
    _L1_xattn_all = _L1_xattn_setup()
    _L1_xattn_in = {k: v for k, v in _L1_xattn_all.items() if k in ('q_w', 'q_b', 'k_w', 'k_b', 'v_w', 'v_b')}
    del _L1_xattn_all

    def _L1_ffn_setup():
        import jax, jax.numpy as jnp
        import numpy as np
        FEATURES = 128
        D_IN = 128

        def fp8_gemm_optimized(x, input_scale, kernel, kernel_scale):
            s_in = input_scale[0]
            s_k = kernel_scale[0]
            x_q = (x.astype(jnp.float32) / s_in).astype(jnp.float8_e4m3fn)
            k_q = (kernel.astype(jnp.float32) / s_k).astype(jnp.float8_e4m3fn)
            y = jnp.dot(x_q.astype(jnp.float32), k_q.astype(jnp.float32), preferred_element_type=jnp.float32)
            return y * (s_in * s_k)
        key = jax.random.key(seed)
        kx, kk, kb = jax.random.split(key, 3)
        x = jax.random.normal(kx, (4, 1024, D_IN), dtype=jnp.float32)
        limit = np.sqrt(6.0 / (D_IN + FEATURES)).astype(np.float32)
        kernel = jax.random.uniform(kk, (D_IN, FEATURES), dtype=jnp.float32, minval=-limit, maxval=limit).astype(jnp.bfloat16)
        input_scale = jnp.ones((1,), dtype=jnp.float32)
        kernel_scale = jnp.ones((1,), dtype=jnp.float32)
        bias = jnp.zeros((FEATURES,), dtype=jnp.bfloat16)
        return {'x': x, 'kernel': kernel, 'input_scale': input_scale, 'kernel_scale': kernel_scale, 'bias': bias}
    _L1_ffn_all = _L1_ffn_setup()
    _L1_ffn_in = {k: v for k, v in _L1_ffn_all.items() if k in ('kernel', 'input_scale', 'kernel_scale', 'bias')}
    del _L1_ffn_all

    def _L2_xattn_setup():
        import jax, jax.numpy as jnp
        import numpy as np
        import math
        D_MODEL = 128
        N_HEADS = 16
        D_HEAD = D_MODEL // N_HEADS
        key = jax.random.key(seed)
        ks = jax.random.split(key, 11)
        N, L, S = (2, 256, 256)
        inp = {'queries': jax.random.normal(ks[0], (N, L, D_MODEL), dtype=jnp.float32), 'keys': jax.random.normal(ks[1], (N, S, D_MODEL), dtype=jnp.float32), 'values': jax.random.normal(ks[2], (N, S, D_MODEL), dtype=jnp.float32), 'Wq': jax.random.normal(ks[3], (D_MODEL, N_HEADS * D_HEAD), dtype=jnp.float32) / math.sqrt(D_MODEL), 'bq': jnp.zeros((N_HEADS * D_HEAD,), dtype=jnp.float32), 'Wk': jax.random.normal(ks[4], (D_MODEL, N_HEADS * D_HEAD), dtype=jnp.float32) / math.sqrt(D_MODEL), 'bk': jnp.zeros((N_HEADS * D_HEAD,), dtype=jnp.float32), 'Wv': jax.random.normal(ks[5], (D_MODEL, N_HEADS * D_HEAD), dtype=jnp.float32) / math.sqrt(D_MODEL), 'bv': jnp.zeros((N_HEADS * D_HEAD,), dtype=jnp.float32), 'Wo': jax.random.normal(ks[6], (N_HEADS * D_HEAD, D_MODEL), dtype=jnp.float32) / math.sqrt(N_HEADS * D_HEAD), 'bo': jnp.zeros((D_MODEL,), dtype=jnp.float32)}
        return inp
    _L2_xattn_all = _L2_xattn_setup()
    _L2_xattn_in = {k: v for k, v in _L2_xattn_all.items() if k in ('Wq', 'bq', 'Wk', 'bk', 'Wv', 'bv', 'Wo', 'bo')}
    del _L2_xattn_all

    def _L2_ffn_setup():
        import jax, jax.numpy as jnp
        import numpy as np
        TOP_K = 2
        key = jax.random.key(seed)
        ks = jax.random.split(key, 6)
        B, T, H, E, F = (2, 256, 128, 8, 512)
        s = 0.02
        return {'hidden_states': jax.random.normal(ks[0], (B, T, H), dtype=jnp.float32), 'router_w': jax.random.normal(ks[1], (E, H), dtype=jnp.float32) * s, 'w1': jax.random.normal(ks[2], (E, F, H), dtype=jnp.float32) * s, 'b1': jax.random.normal(ks[3], (E, F), dtype=jnp.float32) * s, 'w2': jax.random.normal(ks[4], (E, H, F), dtype=jnp.float32) * s, 'b2': jax.random.normal(ks[5], (E, H), dtype=jnp.float32) * s}
    _L2_ffn_all = _L2_ffn_setup()
    _L2_ffn_in = {k: v for k, v in _L2_ffn_all.items() if k in ('router_w', 'w1', 'b1', 'w2', 'b2')}
    del _L2_ffn_all

    def _L3_xattn_setup():
        import jax, jax.numpy as jnp
        import numpy as np
        DIM = 128
        NUM_HEADS = 16
        HEAD_DIM = DIM // NUM_HEADS
        SCALE = HEAD_DIM ** (-0.5)
        key = jax.random.key(seed)
        ks = jax.random.split(key, 10)
        b, nq, nkv = (1, 512, 512)
        s = DIM ** (-0.5)
        return {'q': jax.random.normal(ks[0], (b, nq, DIM), jnp.float32), 'kv': jax.random.normal(ks[1], (b, nkv, DIM), jnp.float32), 'q_w': jax.random.normal(ks[2], (DIM, DIM), jnp.float32) * s, 'q_b': jnp.zeros((DIM,), jnp.float32), 'k_w': jax.random.normal(ks[3], (DIM, DIM), jnp.float32) * s, 'k_b': jnp.zeros((DIM,), jnp.float32), 'v_w': jax.random.normal(ks[4], (DIM, DIM), jnp.float32) * s, 'v_b': jnp.zeros((DIM,), jnp.float32), 'o_w': jax.random.normal(ks[5], (DIM, DIM), jnp.float32) * s, 'o_b': jnp.zeros((DIM,), jnp.float32)}
    _L3_xattn_all = _L3_xattn_setup()
    _L3_xattn_in = {k: v for k, v in _L3_xattn_all.items() if k in ('q_w', 'q_b', 'k_w', 'k_b', 'v_w', 'v_b', 'o_w', 'o_b')}
    del _L3_xattn_all

    def _L3_ffn_setup():
        import jax, jax.numpy as jnp
        import numpy as np
        D, H, E, K, S = (128, 256, 8, 2, 1)
        B, L = (4, 256)
        key = jax.random.key(seed)
        ks = jax.random.split(key, 9)
        std = 0.02
        return {'x': jax.random.normal(ks[0], (B, L, D), dtype=jnp.float32), 'router_w': jax.random.normal(ks[1], (E, D), dtype=jnp.float32) * std, 'experts_bias': jnp.zeros((E,), dtype=jnp.float32), 'w1': jax.random.normal(ks[2], (E, D, H), dtype=jnp.float32) * std, 'w3': jax.random.normal(ks[3], (E, D, H), dtype=jnp.float32) * std, 'w2': jax.random.normal(ks[4], (E, H, D), dtype=jnp.float32) * std, 'sw1': jax.random.normal(ks[5], (S, D, H), dtype=jnp.float32) * std, 'sw3': jax.random.normal(ks[6], (S, D, H), dtype=jnp.float32) * std, 'sw2': jax.random.normal(ks[7], (S, H, D), dtype=jnp.float32) * std}
    _L3_ffn_all = _L3_ffn_setup()
    _L3_ffn_in = {k: v for k, v in _L3_ffn_all.items() if k in ('router_w', 'experts_bias', 'w1', 'w3', 'w2', 'sw1', 'sw3', 'sw2')}
    del _L3_ffn_all
    return {'x': x, 'ctx_1024': ctx_1024, 'mask_BxS2_fk1': mask_BxS2_fk1, 'mask_BxS2_ik0': mask_BxS2_ik0, 'L0_xattn_Wq': _L0_xattn_in['Wq'], 'L0_xattn_Wk': _L0_xattn_in['Wk'], 'L0_xattn_Wv': _L0_xattn_in['Wv'], 'L0_xattn_Wo': _L0_xattn_in['Wo'], 'L0_ffn_rW1': _L0_ffn_in['rW1'], 'L0_ffn_rb1': _L0_ffn_in['rb1'], 'L0_ffn_rW2': _L0_ffn_in['rW2'], 'L0_ffn_rb2': _L0_ffn_in['rb2'], 'L0_ffn_rW3': _L0_ffn_in['rW3'], 'L0_ffn_rb3': _L0_ffn_in['rb3'], 'L0_ffn_eW1': _L0_ffn_in['eW1'], 'L0_ffn_eb1': _L0_ffn_in['eb1'], 'L0_ffn_eW2': _L0_ffn_in['eW2'], 'L0_ffn_eb2': _L0_ffn_in['eb2'], 'L1_xattn_q_w': _L1_xattn_in['q_w'], 'L1_xattn_q_b': _L1_xattn_in['q_b'], 'L1_xattn_k_w': _L1_xattn_in['k_w'], 'L1_xattn_k_b': _L1_xattn_in['k_b'], 'L1_xattn_v_w': _L1_xattn_in['v_w'], 'L1_xattn_v_b': _L1_xattn_in['v_b'], 'L1_ffn_kernel': _L1_ffn_in['kernel'], 'L1_ffn_input_scale': _L1_ffn_in['input_scale'], 'L1_ffn_kernel_scale': _L1_ffn_in['kernel_scale'], 'L1_ffn_bias': _L1_ffn_in['bias'], 'L2_xattn_Wq': _L2_xattn_in['Wq'], 'L2_xattn_bq': _L2_xattn_in['bq'], 'L2_xattn_Wk': _L2_xattn_in['Wk'], 'L2_xattn_bk': _L2_xattn_in['bk'], 'L2_xattn_Wv': _L2_xattn_in['Wv'], 'L2_xattn_bv': _L2_xattn_in['bv'], 'L2_xattn_Wo': _L2_xattn_in['Wo'], 'L2_xattn_bo': _L2_xattn_in['bo'], 'L2_ffn_router_w': _L2_ffn_in['router_w'], 'L2_ffn_w1': _L2_ffn_in['w1'], 'L2_ffn_b1': _L2_ffn_in['b1'], 'L2_ffn_w2': _L2_ffn_in['w2'], 'L2_ffn_b2': _L2_ffn_in['b2'], 'L3_xattn_q_w': _L3_xattn_in['q_w'], 'L3_xattn_q_b': _L3_xattn_in['q_b'], 'L3_xattn_k_w': _L3_xattn_in['k_w'], 'L3_xattn_k_b': _L3_xattn_in['k_b'], 'L3_xattn_v_w': _L3_xattn_in['v_w'], 'L3_xattn_v_b': _L3_xattn_in['v_b'], 'L3_xattn_o_w': _L3_xattn_in['o_w'], 'L3_xattn_o_b': _L3_xattn_in['o_b'], 'L3_ffn_router_w': _L3_ffn_in['router_w'], 'L3_ffn_experts_bias': _L3_ffn_in['experts_bias'], 'L3_ffn_w1': _L3_ffn_in['w1'], 'L3_ffn_w3': _L3_ffn_in['w3'], 'L3_ffn_w2': _L3_ffn_in['w2'], 'L3_ffn_sw1': _L3_ffn_in['sw1'], 'L3_ffn_sw3': _L3_ffn_in['sw3'], 'L3_ffn_sw2': _L3_ffn_in['sw2']}

def reference(x, ctx_1024, mask_BxS2_fk1, mask_BxS2_ik0, L0_xattn_Wq, L0_xattn_Wk, L0_xattn_Wv, L0_xattn_Wo, L0_ffn_rW1, L0_ffn_rb1, L0_ffn_rW2, L0_ffn_rb2, L0_ffn_rW3, L0_ffn_rb3, L0_ffn_eW1, L0_ffn_eb1, L0_ffn_eW2, L0_ffn_eb2, L1_xattn_q_w, L1_xattn_q_b, L1_xattn_k_w, L1_xattn_k_b, L1_xattn_v_w, L1_xattn_v_b, L1_ffn_kernel, L1_ffn_input_scale, L1_ffn_kernel_scale, L1_ffn_bias, L2_xattn_Wq, L2_xattn_bq, L2_xattn_Wk, L2_xattn_bk, L2_xattn_Wv, L2_xattn_bv, L2_xattn_Wo, L2_xattn_bo, L2_ffn_router_w, L2_ffn_w1, L2_ffn_b1, L2_ffn_w2, L2_ffn_b2, L3_xattn_q_w, L3_xattn_q_b, L3_xattn_k_w, L3_xattn_k_b, L3_xattn_v_w, L3_xattn_v_b, L3_xattn_o_w, L3_xattn_o_b, L3_ffn_router_w, L3_ffn_experts_bias, L3_ffn_w1, L3_ffn_w3, L3_ffn_w2, L3_ffn_sw1, L3_ffn_sw3, L3_ffn_sw2):
    import jax
    import jax.numpy as jnp

    def _L0_xattn_ref(queries, keys, values, ind_q, ind_k, ind_v, Wq, Wk, Wv, Wo):
        import jax, jax.numpy as jnp
        import numpy as np
        B, S, D = (2, 256, 128)
        H, HD = (16, 64)
        b, nq, _ = queries.shape
        nk = keys.shape[1]
        Q = (queries @ Wq).reshape(b, nq, H, HD).transpose(0, 2, 1, 3) * ind_q[:, None, :, None]
        K = (keys @ Wk).reshape(b, nk, H, HD).transpose(0, 2, 1, 3) * ind_k[:, None, :, None]
        V = (values @ Wv).reshape(b, nk, H, HD).transpose(0, 2, 1, 3) * ind_v[:, None, :, None]
        scores = jnp.einsum('bhqd,bhkd->bhqk', Q, K) / jnp.sqrt(jnp.float32(HD))
        attn = jax.nn.softmax(scores, axis=-1)
        attn = attn * ind_k[:, None, None, :]
        denom = jnp.sum(attn, axis=-1, keepdims=True)
        attn = attn / jnp.where(denom == 0.0, 1.0, denom)
        out = jnp.einsum('bhqk,bhkd->bhqd', attn, V)
        out = out.transpose(0, 2, 1, 3).reshape(b, nq, H * HD)
        return out @ Wo

    def _L0_ffn_ref(x, rW1, rb1, rW2, rb2, rW3, rb3, eW1, eb1, eW2, eb2):
        import jax, jax.numpy as jnp
        import numpy as np
        N_EMBD = 128
        N_EXPERTS = 8
        TOP_K = 2
        CAPACITY_FACTOR = 1.25
        B, T, C = x.shape
        E = rb3.shape[0]
        k = TOP_K
        capacity = int(T / E * CAPACITY_FACTOR)
        h = jax.nn.relu(x @ rW1 + rb1)
        h = jax.nn.relu(h @ rW2 + rb2)
        scales = jax.nn.softmax(h @ rW3 + rb3, axis=-1)
        topk_scales, topk_experts = jax.lax.top_k(scales, k)
        e_flat = topk_experts.reshape(B, T * k)
        onehot = jax.nn.one_hot(e_flat, E, dtype=jnp.int32)
        pos_excl = jnp.cumsum(onehot, axis=1) - onehot
        pos = jnp.take_along_axis(pos_excl, e_flat[..., None], axis=-1)[..., 0]
        keep = pos < capacity
        pos_c = jnp.where(keep, pos, capacity)
        b_idx = jnp.broadcast_to(jnp.arange(B)[:, None], (B, T * k))
        x_rep = jnp.repeat(x, k, axis=1)
        dispatched = jnp.zeros((E, B, capacity, C), x.dtype)
        dispatched = dispatched.at[e_flat, b_idx, pos_c].set(jnp.where(keep[..., None], x_rep, 0.0), mode='drop')
        hh = jax.nn.relu(jnp.einsum('ebnc,ech->ebnh', dispatched, eW1) + eb1[:, None, None, :])
        eout = jnp.einsum('ebnh,ehc->ebnc', hh, eW2) + eb2[:, None, None, :]
        gathered = eout[e_flat, b_idx, pos_c]
        gathered = jnp.where(keep[..., None], gathered, 0.0).reshape(B, T, k, C)
        out = jnp.sum(topk_scales[..., None] * gathered, axis=2)
        return out

    def _L1_xattn_ref(hidden_states, context, attention_mask, q_w, q_b, k_w, k_b, v_w, v_b):
        import jax, jax.numpy as jnp
        import numpy as np
        B, LQ, LK, D = (4, 256, 256, 128)
        H = 16
        HD = D // H

        def _split_heads(x):
            b, l, _ = x.shape
            return x.reshape(b, l, H, HD).transpose(0, 2, 1, 3)
        q = _split_heads(hidden_states @ q_w.T + q_b)
        k = _split_heads(context @ k_w.T + k_b)
        v = _split_heads(context @ v_w.T + v_b)
        scores = jnp.einsum('bhqd,bhkd->bhqk', q, k) / jnp.sqrt(jnp.float32(HD))
        mask = (attention_mask > 0)[:, None, None, :]
        scores = jnp.where(mask, -jnp.inf, scores)
        probs = jax.nn.softmax(scores, axis=-1)
        ctx = jnp.einsum('bhqk,bhkd->bhqd', probs, v)
        ctx = ctx.transpose(0, 2, 1, 3).reshape(ctx.shape[0], ctx.shape[2], H * HD)
        return ctx

    def _L1_ffn_ref(x, kernel, input_scale, kernel_scale, bias):
        import jax, jax.numpy as jnp
        import numpy as np
        FEATURES = 128
        D_IN = 128

        def fp8_gemm_optimized(x, input_scale, kernel, kernel_scale):
            s_in = input_scale[0]
            s_k = kernel_scale[0]
            x_q = (x.astype(jnp.float32) / s_in).astype(jnp.float8_e4m3fn)
            k_q = (kernel.astype(jnp.float32) / s_k).astype(jnp.float8_e4m3fn)
            y = jnp.dot(x_q.astype(jnp.float32), k_q.astype(jnp.float32), preferred_element_type=jnp.float32)
            return y * (s_in * s_k)
        dtype = jnp.bfloat16
        x = x.astype(dtype)
        orig_shape = x.shape
        x2 = x.reshape(-1, x.shape[-1])
        y = fp8_gemm_optimized(x2, input_scale, kernel, kernel_scale)
        y = y.astype(dtype) + bias
        return y.reshape(orig_shape[:-1] + (FEATURES,))

    def _L2_xattn_ref(queries, keys, values, Wq, bq, Wk, bk, Wv, bv, Wo, bo):
        import jax, jax.numpy as jnp
        import numpy as np
        import math
        D_MODEL = 128
        N_HEADS = 16
        D_HEAD = D_MODEL // N_HEADS
        N, L, _ = queries.shape
        S = keys.shape[1]
        H, D = (N_HEADS, D_HEAD)
        q = (queries @ Wq + bq).reshape(N, L, H, D)
        k = (keys @ Wk + bk).reshape(N, S, H, D)
        v = (values @ Wv + bv).reshape(N, S, H, D)
        sm = jnp.einsum('nlhd,nshd->nlhs', q, k) / math.sqrt(D)
        sm = jax.nn.softmax(sm, axis=1)
        attn = jnp.einsum('nlhs,nshd->nlhd', sm, v).reshape(N, L, H * D)
        return attn @ Wo + bo

    def _L2_ffn_ref(hidden_states, router_w, w1, b1, w2, b2):
        import jax, jax.numpy as jnp
        import numpy as np
        TOP_K = 2
        x = hidden_states
        router_logits = jnp.einsum('bth,eh->bte', x, router_w)
        topk_values, topk_indices = jax.lax.top_k(router_logits, TOP_K)
        topk_weights = jax.nn.softmax(topk_values.astype(jnp.float32), axis=-1).astype(x.dtype)
        h1 = jnp.einsum('bth,efh->btef', x, w1) + b1
        h1 = jax.nn.gelu(h1, approximate=False)
        expert_outputs = jnp.einsum('btef,ehf->bteh', h1, w2) + b2
        gather_idx = topk_indices[..., None]
        topk_expert_outputs = jnp.take_along_axis(expert_outputs, gather_idx, axis=2)
        mixed_output = jnp.sum(topk_expert_outputs * topk_weights[..., None], axis=2)
        return mixed_output

    def _L3_xattn_ref(q, kv, q_w, q_b, k_w, k_b, v_w, v_b, o_w, o_b):
        import jax, jax.numpy as jnp
        import numpy as np
        DIM = 128
        NUM_HEADS = 16
        HEAD_DIM = DIM // NUM_HEADS
        SCALE = HEAD_DIM ** (-0.5)
        b, nq, _ = q.shape
        nkv = kv.shape[1]
        h, c = (NUM_HEADS, HEAD_DIM)
        qh = (q @ q_w.T + q_b).reshape(b, nq, h, c).transpose(0, 2, 1, 3)
        kh = (kv @ k_w.T + k_b).reshape(b, nkv, h, c).transpose(0, 2, 1, 3)
        vh = (kv @ v_w.T + v_b).reshape(b, nkv, h, c).transpose(0, 2, 1, 3)
        attn = jnp.einsum('bhqc,bhkc->bhqk', qh, kh) * SCALE
        attn = jax.nn.softmax(attn, axis=-1)
        out = jnp.einsum('bhqk,bhkc->bhqc', attn, vh)
        out = out.transpose(0, 2, 1, 3).reshape(b, nq, h * c)
        out = out @ o_w.T + o_b
        return out

    def _L3_ffn_ref(x, router_w, experts_bias, w1, w3, w2, sw1, sw3, sw2):
        import jax, jax.numpy as jnp
        import numpy as np
        D, H, E, K, S = (128, 256, 8, 2, 1)
        B, L = (4, 256)
        b, l, d = x.shape
        xf = x.reshape(-1, d)
        sg = jnp.einsum('td,sdh->tsh', xf, sw1)
        su = jnp.einsum('td,sdh->tsh', xf, sw3)
        shared_out = jnp.einsum('tsh,shd->td', jax.nn.silu(sg) * su, sw2)
        logits = xf @ router_w.T + experts_bias
        rw, sel = jax.lax.top_k(logits, K)
        rw = jax.nn.softmax(rw.astype(jnp.float32), axis=-1).astype(x.dtype)
        cw = (jax.nn.one_hot(sel, E, dtype=x.dtype) * rw[..., None]).sum(axis=1)
        g = jnp.einsum('td,edh->teh', xf, w1)
        u = jnp.einsum('td,edh->teh', xf, w3)
        eo = jax.nn.silu(g) * u
        moe_out = jnp.einsum('te,teh,ehd->td', cw, eo, w2)
        return (moe_out + shared_out).reshape(b, l, d)
    x = x + _L0_xattn_ref(_layernorm(x, axis=-1), ctx_1024, ctx_1024, mask_BxS2_fk1, mask_BxS2_fk1, mask_BxS2_fk1, L0_xattn_Wq, L0_xattn_Wk, L0_xattn_Wv, L0_xattn_Wo)
    x = x + _L0_ffn_ref(_layernorm(x, axis=-1), L0_ffn_rW1, L0_ffn_rb1, L0_ffn_rW2, L0_ffn_rb2, L0_ffn_rW3, L0_ffn_rb3, L0_ffn_eW1, L0_ffn_eb1, L0_ffn_eW2, L0_ffn_eb2)
    x = x + _L1_xattn_ref(_layernorm(x, axis=-1), ctx_1024, mask_BxS2_ik0, L1_xattn_q_w, L1_xattn_q_b, L1_xattn_k_w, L1_xattn_k_b, L1_xattn_v_w, L1_xattn_v_b)
    x = x + _L1_ffn_ref(_layernorm(x, axis=-1), L1_ffn_kernel, L1_ffn_input_scale, L1_ffn_kernel_scale, L1_ffn_bias)
    x = x + _L2_xattn_ref(_layernorm(x, axis=-1), ctx_1024, ctx_1024, L2_xattn_Wq, L2_xattn_bq, L2_xattn_Wk, L2_xattn_bk, L2_xattn_Wv, L2_xattn_bv, L2_xattn_Wo, L2_xattn_bo)
    x = x + _L2_ffn_ref(_layernorm(x, axis=-1), L2_ffn_router_w, L2_ffn_w1, L2_ffn_b1, L2_ffn_w2, L2_ffn_b2)
    x = x + _L3_xattn_ref(_layernorm(x, axis=-1), ctx_1024, L3_xattn_q_w, L3_xattn_q_b, L3_xattn_k_w, L3_xattn_k_b, L3_xattn_v_w, L3_xattn_v_b, L3_xattn_o_w, L3_xattn_o_b)
    x = x + _L3_ffn_ref(_layernorm(x, axis=-1), L3_ffn_router_w, L3_ffn_experts_bias, L3_ffn_w1, L3_ffn_w3, L3_ffn_w2, L3_ffn_sw1, L3_ffn_sw3, L3_ffn_sw2)
    return x

_drawn_inputs = setup_inputs


def setup_inputs(seed=0):
    import zlib

    import numpy as np

    out = dict(_drawn_inputs(seed))
    spreads = {'L0_ffn_rb1': (0.0, 0.8),
     'L0_ffn_rb2': (0.0, 0.635),
     'L0_ffn_rb3': (0.0, 0.472),
     'L0_ffn_eb1': (0.0, 0.8),
     'L0_ffn_eb2': (0.0, 0.742),
     'L1_xattn_q_b': (0.0, 0.8),
     'L1_xattn_k_b': (0.0, 0.8),
     'L1_xattn_v_b': (0.0, 0.1),
     'L1_ffn_bias': (0.0, 0.1),
     'L2_xattn_bq': (0.0, 0.8),
     'L2_xattn_bk': (0.0, 0.1),
     'L2_xattn_bv': (0.0, 0.1),
     'L2_xattn_bo': (0.0, 0.1),
     'L3_xattn_q_b': (0.0, 0.666),
     'L3_xattn_k_b': (0.0, 0.8),
     'L3_xattn_v_b': (0.0, 0.1),
     'L3_xattn_o_b': (0.0, 0.1),
     'L3_ffn_experts_bias': (0.0, 0.8)}
    factors = {'L0_ffn_rW1': 6.653,
     'L0_ffn_rW2': 7.212,
     'L0_ffn_rW3': 5.508,
     'L0_ffn_eW1': 7.939,
     'L0_ffn_eW2': 6.589,
     'L1_xattn_q_w': 8.0,
     'L1_xattn_k_w': 8.0,
     'L2_ffn_router_w': 2.79,
     'L2_ffn_b1': 8.0,
     'L2_ffn_b2': 6.79,
     'L3_ffn_router_w': 8.0,
     'L3_ffn_w1': 8.0,
     'L3_ffn_w3': 8.0,
     'L3_ffn_w2': 8.0,
     'L3_ffn_sw1': 8.0,
     'L3_ffn_sw3': 8.0,
     'L3_ffn_sw2': 8.0}
    for name, (base, spread) in spreads.items():
        noise = np.random.default_rng([zlib.crc32(name.encode()), seed]).standard_normal(out[name].shape)
        drawn = base * np.exp(spread * noise) if base else spread * noise
        out[name] = jnp.asarray(drawn.astype(out[name].dtype))
    for name, factor in factors.items():
        out[name] = (out[name] * factor).astype(out[name].dtype)
    return out
```

```python
from contextlib import ExitStack

import numpy as np

import concourse.bass as bass
from concourse import mybir

F32 = mybir.dt.float32
BF16 = mybir.dt.bfloat16
U32 = mybir.dt.uint32
I32 = mybir.dt.int32
ALU = mybir.AluOpType
ACT = mybir.ActivationFunctionType
AX = mybir.AxisListType.X

P = 128
SEQ = 64
D = 128
TOKENS = 64 * SEQ
TILES = TOKENS // P
HEADS = 16
PAIRS = HEADS // 2
UNIT = 4
UNITS = TILES // UNIT
UTOK = UNIT * P
EXPERTS = 8
BANKS = 8
DMA_INC = 16
EPS = 1e-5
CAPACITY = int(SEQ / EXPERTS * 1.25)
MASKED = -1e30


GROUPS = {
    "ctx": [("ident", [P, P], F32), ("ctx_t", [P, TILES, P], F32)],
    "wide": [("mask_f_col", [P, TILES], F32), ("mask_f_keys", [P, TILES, SEQ], F32),
             ("wide_wq", [P, 1024], F32), ("wide_wk", [P, 1024], F32), ("wide_wv", [P, 1024], F32),
             ("wide_wo", [P, 8, P], F32)],
    "const": [("head_mask", [P, HEADS], F32), ("batch_mask", [P, 2], F32), ("block_mask", [P, 4], F32),
              ("half_ones", [P, 32], F32)],
    "mask_i": [("mask_i_keys", [P, TILES, SEQ], I32)],
    "attn1": [("attn1_wq", [P, P], F32), ("attn1_wk", [P, P], F32), ("attn1_wv", [P, P], F32),
              ("attn1_wo", [P, 2, P], F32), ("attn1_bq", [P, 1], F32), ("attn1_bk", [P, 1], F32),
              ("attn1_bo", [P, P], F32)],
    "attn2": [("attn2_wq", [P, P], F32), ("attn2_wk", [P, P], F32), ("attn2_wv", [P, P], F32),
              ("attn2_wo", [P, 2, P], F32), ("attn2_bq", [P, 1], F32), ("attn2_bk", [P, 1], F32),
              ("attn2_bv", [P, P], F32), ("attn2_bo", [P, P], F32)],
    "attn3": [("attn3_wq", [P, P], F32), ("attn3_wk", [P, P], F32), ("attn3_wv", [P, P], F32),
              ("attn3_wo", [P, 2, P], F32), ("attn3_wo_plain", [P, P], F32), ("attn3_bq", [P, 1], F32),
              ("attn3_bk", [P, 1], F32), ("attn3_bv", [P, P], F32), ("attn3_bo", [P, P], F32)],
    "moe_const": [("numbers", [P, EXPERTS], F32), ("earlier", [P, P], F32)],
    "moe0": [("moe0_rw1", [P, 512], F32), ("moe0_rb1", [P, 4], F32), ("moe0_rw2", [P, 4, 512], F32),
             ("moe0_rb2", [P, 4], F32), ("moe0_rw", [P, 4, EXPERTS], F32), ("moe0_rb", [EXPERTS, 1], F32),
             ("moe0_w1", [P, EXPERTS, 512], F32), ("moe0_b1", [P, 4 * EXPERTS], F32),
             ("moe0_w2", [P, EXPERTS, 4, P], F32), ("moe0_b2", [EXPERTS, P], F32)],
    "moe2": [("moe2_rw", [P, EXPERTS], F32), ("moe2_w1", [P, EXPERTS, 512], F32), ("moe2_b1", [P, 4 * EXPERTS], F32),
             ("moe2_w2", [P, EXPERTS, 4, P], F32), ("moe2_b2", [EXPERTS, P], F32)],
    "moe3": [("moe3_rw", [P, EXPERTS], F32), ("moe3_rb", [EXPERTS, 1], F32), ("moe3_w1", [P, EXPERTS + 1, 256], F32),
             ("moe3_w3", [P, EXPERTS + 1, 256], F32), ("moe3_w2", [P, EXPERTS + 1, 2, P], F32)],
    "fp8": [("fp8_kernel", [P, P], BF16), ("fp8_scales", [P, 2], F32), ("fp8_bias", [P, P], BF16)],
}


class Step:

    def __init__(self, i, off, stride=2):
        self.i, self.off, self.stride = i, off, stride

    def minus(self, n):
        return Step(self.i, self.off - n, self.stride)

    def at(self, k, c):
        rest = k * self.off + c
        if self.i is None:
            return rest
        by = self.i * (self.stride * k)
        return by + rest if rest >= 0 else by - (-rest)

    def inside(self, n):
        return self.i is not None or 0 <= self.off < n

    def past(self, n):
        return self.i is not None or self.off >= n

    @property
    def parity(self):
        return self.off % 2


def pipelined(eng, n, lag, body):
    first = lag + lag % 2
    for s in range(first):
        body(Step(None, s))
    with eng.Fori(first // 2, n // 2) as i:
        for off in range(2):
            body(Step(i, off))
    for s in range(n, n + lag):
        body(Step(None, s))


def tile_of(buffer, u, k=1, c=0):
    at = u.at(k, c)
    if isinstance(at, int):
        return buffer[:, at, :]
    return buffer[:, bass.ds(at, 1), :].rearrange("p a c -> p (a c)")


class Core:

    def __init__(self, nc, stack, args):
        self.nc, self.stack, self.args = nc, stack, args
        self.bank = [stack.enter_context(nc.psum_tensor(f"bank{n}", [P, 512], F32)) for n in range(BANKS)]
        self.x = self.sb("x", [P, TILES, D])
        self.stats = self.sb("stats", [P, TILES, 6])
        self.mean = self.sb("mean", [P, TILES])
        self.rstd = self.sb("rstd", [P, TILES])
        self.apart, self.std, self.half, self.var = (self.sb("norm_" + n, [P, TILES]) for n in ("apart", "std", "half", "var"))
        self.var_ready, self.std_ready, self.newton = (self.sem("norm_" + n) for n in ("var_ready", "std_ready", "newton"))
        self.stage_sems = []
        self.w, self.groups, self.loaded, self.loads = {}, {}, {}, {}

    def sb(self, name, shape, dt=F32, stack=None):
        return (stack or self.stack).enter_context(self.nc.sbuf_tensor(name, shape, dt))

    def sem(self, name):
        return self.stack.enter_context(self.nc.semaphore(name))

    def stage_sem(self, name):
        self.stage_sems.append(self.nc.alloc_semaphore(name=name))
        return self.stage_sems[-1]

    def end_of_stage(self):
        self.nc.clear_and_free_semaphores(self.stage_sems)
        self.nc.all_engine_barrier()
        self.stage_sems = []


def token_stats(core, dve, ready, u):
    dve.wait_ge(ready, u.at(1, 1))
    dve.wait_ge(ready, 1)
    core.nc.vector.bn_stats(tile_of(core.stats, u), tile_of(core.x, u))


def add_and_norm(core, dve, added, u, y, base):
    x_u = tile_of(core.x, u)
    core.nc.vector.tensor_tensor(x_u, y, base if base is not None else x_u, ALU.add).then_inc(added, 1)
    token_stats(core, dve, added, u)


def norm_scale(core, nth):
    nc = core.nc
    even, odd = core.stats[:, :, 1], core.stats[:, :, 4]
    even_sq, odd_sq = core.stats[:, :, 2], core.stats[:, :, 5]
    apart, std, half, var = core.apart, core.std, core.half, core.var
    var_ready, std_ready, newton = core.var_ready, core.std_ready, core.newton
    with nc.Block() as block:

        @block.vector
        def _(dve):
            nc.vector.tensor_tensor(core.mean[:], even, odd, ALU.add)
            nc.vector.tensor_tensor(apart[:], even, odd, ALU.subtract)
            nc.vector.tensor_tensor(var[:], even_sq, odd_sq, ALU.add).then_inc(var_ready, 1)
            dve.wait_ge(var_ready, 4 * nth + 1)
            nc.vector.tensor_scalar(core.mean[:], core.mean[:], 0.5, None, ALU.mult)
            nc.vector.tensor_scalar(apart[:], apart[:], 0.5, None, ALU.mult)
            nc.vector.tensor_scalar(var[:], var[:], 1.0 / D, EPS, ALU.mult, ALU.add).then_inc(var_ready, 1)
            dve.wait_ge(var_ready, 4 * nth + 2)
            nc.vector.tensor_tensor(apart[:], apart[:], apart[:], ALU.mult).then_inc(var_ready, 1)
            dve.wait_ge(var_ready, 4 * nth + 3)
            nc.vector.tensor_tensor(var[:], var[:], apart[:], ALU.add).then_inc(var_ready, 1)
            dve.wait_ge(std_ready, nth + 1)
            nc.vector.reciprocal(core.rstd[:], std[:]).then_inc(newton, 1)
            dve.wait_ge(newton, 4 * nth + 1)
            nc.vector.tensor_tensor(half[:], core.rstd[:], core.rstd[:], ALU.mult).then_inc(newton, 1)
            dve.wait_ge(newton, 4 * nth + 2)
            nc.vector.tensor_tensor(half[:], half[:], var[:], ALU.mult).then_inc(newton, 1)
            dve.wait_ge(newton, 4 * nth + 3)
            nc.vector.tensor_scalar(half[:], half[:], -0.5, 1.5, ALU.mult, ALU.add).then_inc(newton, 1)
            dve.wait_ge(newton, 4 * nth + 4)
            nc.vector.tensor_tensor(core.rstd[:], core.rstd[:], half[:], ALU.mult)

        @block.scalar
        def _(act):
            act.wait_ge(var_ready, 4 * nth + 4)
            nc.scalar.activation(std[:], var[:], ACT.Sqrt).then_inc(std_ready, 1)


def normalize(core, u, out, rstd, sem, k=1, c=0):
    at = u.at(k, c)
    one = slice(at, at + 1) if isinstance(at, int) else bass.ds(at, 1)
    ins = core.nc.vector.tensor_scalar(out, tile_of(core.x, u, k, c), core.mean[:, one], rstd[:, one],
                                       ALU.subtract, ALU.mult)
    if sem is not None:
        ins.then_inc(sem, 1)


def allocate(core, names, stack=None):
    for group in names:
        core.groups[group] = GROUPS[group]
        core.loaded[group] = core.sem("loaded_" + group)
        core.loads[group] = DMA_INC * len(GROUPS[group])
        for name, shape, dt in GROUPS[group]:
            core.w[name] = core.sb(name + "_sb", shape, dt, stack)


def start_loads(core, queue, names):
    for group in names:
        for name, _, _ in GROUPS[group]:
            queue.dma_start(core.w[name][:], core.args[name]).then_inc(core.loaded[group], DMA_INC)


def arrived(core, eng, *names):
    for group in names:
        eng.wait_ge(core.loaded[group], core.loads[group])


def load_and_first_stats(core, names):
    nc, args = core.nc, core.args
    loaded_x = core.sem("loaded_x")
    with nc.Block() as block:

        @block.sync
        def _(sp):
            sp.dma_start(core.x[:], args["x"].rearrange("(t p) c -> p t c", p=P)).then_inc(loaded_x, DMA_INC)
            start_loads(core, sp, names)

        @block.vector
        def _(dve):
            dve.wait_ge(loaded_x, DMA_INC)

            def body(u):
                nc.vector.bn_stats(tile_of(core.stats, u), tile_of(core.x, u))

            pipelined(dve, TILES, 0, body)


def wide_attention(core):
    nc, args, w = core.nc, core.args, core.w
    hd = 64
    scale = hd ** -0.5
    groups = HEADS * hd // P
    with ExitStack() as stack:
        sb = lambda name, shape: core.sb("wide_" + name, shape, stack=stack)
        sem = lambda name: core.stage_sem("wide_" + name)
        xhat = [sb(f"xhat{n}", [P, P]) for n in range(2)]
        x_t = sb("x_t", [P, P])
        mask_row = [sb(f"mask_row{n}", [P, P]) for n in range(2)]
        ctx_m = [sb(f"ctx_m{n}", [P, P]) for n in range(2)]
        q_t = sb("q_t", [P, groups, P])
        k_bd = sb("k_bd", [P, 2, PAIRS, 2, SEQ])
        v_bd = [sb(f"v_bd{n}", [P, 2, PAIRS, 2, hd]) for n in range(2)]
        probs = sb("probs", [P, HEADS, SEQ])
        top = sb("top", [P, HEADS])
        total = sb("total", [P, HEADS])
        total_safe = sb("total_safe", [P, HEADS])
        inverse = [sb(f"inverse{n}", [P, HEADS]) for n in range(2)]
        probs_t = sb("probs_t", [P, PAIRS, P])
        heads_out = sb("heads_out", [P, HEADS, hd])
        heads_t = sb("heads_t", [P, groups, P])
        query_scale = sb("query_scale", [P, TILES])
        query_ready = sem("query_ready")

        mask_landed = [sem(f"mask_landed{n}") for n in range(2)]
        mask_used = sem("ctx_masked")
        zeroed_k, zeroed_v = sem("zeroed_k"), sem("zeroed_v")
        xhat_ready = sem("xhat_ready")
        xt_made, xt_taken = sem("xt_made"), sem("xt_taken")
        projected = sem("projected")
        qk_taken, v_taken = sem("qk_taken"), sem("v_taken")
        scored, top_ready, shifted = sem("scored"), sem("top_ready"), sem("shifted")
        exped, masked = sem("exped"), sem("masked")
        summed, safe, inverted = sem("summed"), sem("safe"), sem("inverted")
        pt_made, pt_taken = sem("pt_made"), sem("pt_taken")
        headed, normed = sem("headed"), sem("normed")
        ht_made, ht_taken = sem("ht_made"), sem("ht_taken")
        made_y = sem("made_y")
        added = sem("added")

        t_bank = core.bank[0:2]
        p_bank = core.bank[2:4]
        o_bank = core.bank[4:6]
        s_bank = core.bank[6:8]

        with nc.Block() as block:

            @block.sync
            def _(sp):
                def body(s):
                    if s.inside(TILES):
                        if s.past(2):
                            sp.wait_ge(mask_used, s.at(1, -1))
                        at = s.at(1, 0)
                        row = args["mask_f_rows"][at:at + 1, :] if isinstance(at, int) else \
                            args["mask_f_rows"][bass.ds(at, 1), :]
                        sp.dma_start(mask_row[s.parity][:], row.to_broadcast([P, P])).then_inc(mask_landed[s.parity], DMA_INC)
                pipelined(sp, TILES, 2, body)

            @block.gpsimd
            def _(pool):
                nc.gpsimd.memset(v_bd[0][:], 0.0)
                nc.gpsimd.memset(v_bd[1][:], 0.0).then_inc(zeroed_v, 1)
                arrived(core, pool, "ctx", "wide")

                def body(s):
                    if s.inside(TILES):
                        pool.wait_ge(mask_landed[s.parity], s.minus(s.parity).at(DMA_INC // 2, DMA_INC))
                        if s.past(2):
                            pool.wait_ge(projected, s.at(6, -6))
                        nc.gpsimd.tensor_tensor(ctx_m[s.parity][:], tile_of(w["ctx_t"], s), mask_row[s.parity][:],
                                                ALU.mult).then_inc(mask_used, 1)
                    u = s.minus(1)
                    if u.inside(TILES):
                        pool.wait_ge(exped, u.at(1, 1))
                        keys = tile_of(w["mask_f_keys"], u).unsqueeze(1).to_broadcast([P, HEADS, SEQ])
                        nc.gpsimd.tensor_tensor(probs[:], probs[:], keys, ALU.mult).then_inc(masked, 1)
                pipelined(pool, TILES, 2, body)

            @block.vector
            def _(dve):
                nc.vector.memset(k_bd[:], 0.0).then_inc(zeroed_k, 1)
                arrived(core, dve, "wide")
                nc.vector.tensor_tensor(query_scale[:], core.rstd[:], w["mask_f_col"][:], ALU.mult
                                        ).then_inc(query_ready, 1)
                dve.wait_ge(query_ready, 1)
                dve.wait_ge(zeroed_v, 1)

                def body(s):
                    if s.inside(TILES):
                        if s.past(2):
                            dve.wait_ge(xt_made, s.at(1, -1))
                        normalize(core, s, xhat[s.parity][:], query_scale, xhat_ready)
                    u = s.minus(1)
                    if u.inside(TILES):
                        dve.wait_ge(scored, u.at(2, 1))
                        for half in range(2):
                            if half == 1:
                                dve.wait_ge(scored, u.at(2, 2))
                            nc.vector.tensor_reduce(
                                top[:, 8 * half:8 * half + 8],
                                s_bank[half][:].rearrange("p (h k) -> p h k", k=SEQ), AX, ALU.max
                            ).then_inc(top_ready, 1)
                        dve.wait_ge(top_ready, u.at(2, 2))
                        for half in range(2):
                            h = slice(8 * half, 8 * half + 8)
                            nc.vector.tensor_tensor(
                                probs[:, h, :], s_bank[half][:].rearrange("p (h k) -> p h k", k=SEQ),
                                top[:, h].unsqueeze(2).to_broadcast([P, 8, SEQ]), ALU.subtract
                            ).then_inc(shifted, 1)
                    u = s.minus(2)
                    if u.inside(TILES):
                        dve.wait_ge(inverted, u.at(1, 1))
                        for half in range(2):
                            h = slice(8 * half, 8 * half + 8)
                            dve.wait_ge(headed, u.at(2, 1 + half))
                            nc.vector.tensor_tensor(
                                heads_out[:, h, :], o_bank[half][:].rearrange("p (h d) -> p h d", d=hd),
                                inverse[u.parity][:, h].unsqueeze(2).to_broadcast([P, 8, hd]), ALU.mult
                            ).then_inc(normed, 1)
                    if s.inside(TILES):
                        for n in range(2):
                            dve.wait_ge(projected, s.at(6, 5 + n))
                            v = p_bank[n][:].rearrange("p (hp h d) -> p hp h d", h=2, d=hd)
                            for b in range(2):
                                for h2 in range(2):
                                    ins = nc.vector.tensor_copy(
                                        v_bd[s.parity][SEQ * h2:SEQ * h2 + SEQ, b, 4 * n:4 * n + 4, h2, :],
                                        v[SEQ * b:SEQ * b + SEQ, :, h2, :])
                            ins.then_inc(v_taken, 1)
                    u = s.minus(1)
                    if u.inside(TILES):
                        dve.wait_ge(masked, u.at(1, 1))
                        nc.vector.tensor_reduce(total[:], probs[:], AX, ALU.add).then_inc(summed, 1)
                        dve.wait_ge(summed, u.at(1, 1))
                        nc.vector.scalar_tensor_tensor(total_safe[:], total[:], 0.0, total[:], ALU.is_equal, ALU.add
                                                       ).then_inc(safe, 1)
                        dve.wait_ge(safe, u.at(1, 1))
                        nc.vector.reciprocal(inverse[u.parity][:], total_safe[:]).then_inc(inverted, 1)
                    u = s.minus(2)
                    if u.inside(TILES):
                        dve.wait_ge(made_y, u.at(1, 1))
                        add_and_norm(core, dve, added, u, o_bank[0][:, 0:P], None)
                pipelined(dve, TILES, 2, body)

            @block.scalar
            def _(act):
                act.wait_ge(zeroed_k, 1)

                def body(s):
                    if s.inside(TILES):
                        act.wait_ge(xt_made, s.at(1, 1))
                        nc.scalar.copy(x_t[:], t_bank[0][:, 0:P]).then_inc(xt_taken, 1)
                        for n in range(2):
                            act.wait_ge(projected, s.at(6, 1 + n))
                            nc.scalar.copy(q_t[:, 4 * n:4 * n + 4, :].rearrange("p g t -> p (g t)"), p_bank[n][:]
                                           ).then_inc(qk_taken, 1)
                    u = s.minus(1)
                    if u.inside(TILES):
                        act.wait_ge(shifted, u.at(2, 2))
                        nc.scalar.activation(probs[:], probs[:], ACT.Exp, scale=scale).then_inc(exped, 1)
                    if s.inside(TILES):
                        for n in range(2):
                            act.wait_ge(projected, s.at(6, 3 + n))
                            k = p_bank[n][:].rearrange("p (hp b k) -> p b hp k", b=2, k=SEQ)
                            for h2 in range(2):
                                rows = slice(SEQ * h2, SEQ * h2 + SEQ)
                                ins = nc.scalar.copy(k_bd[rows, :, 4 * n:4 * n + 4, h2, :], k[rows])
                            ins.then_inc(qk_taken, 1)
                    u = s.minus(2)
                    if u.inside(TILES):
                        for n in range(2):
                            act.wait_ge(ht_made, u.at(2, 1 + n))
                            nc.scalar.copy(heads_t[:, 4 * n:4 * n + 4, :].rearrange("p g t -> p (g t)"),
                                           t_bank[1 - n][:]).then_inc(ht_taken, 1)
                    u = s.minus(1)
                    if u.inside(TILES):
                        for n in range(2):
                            act.wait_ge(pt_made, u.at(2, 1 + n))
                            nc.scalar.copy(probs_t[:, 4 * n:4 * n + 4, :].rearrange("p g t -> p (g t)"),
                                           t_bank[1 - n][:]).then_inc(pt_taken, 1)
                pipelined(act, TILES, 2, body)

            @block.tensor
            def _(pe):
                arrived(core, pe, "ctx", "wide")

                def body(s):
                    two = s.minus(2)
                    one = s.minus(1)
                    if s.inside(TILES):
                        pe.wait_ge(xhat_ready, s.at(1, 1))
                        if s.past(2):
                            pe.wait_ge(pt_taken, s.at(2, -2))
                        nc.tensor.transpose(t_bank[0][:, 0:P], xhat[s.parity][:], w["ident"][:]).then_inc(xt_made, 1)
                        pe.wait_ge(xt_taken, s.at(1, 1))
                        for n in range(2):
                            if s.past(1):
                                pe.wait_ge(v_taken, s.at(2, -1 + n))
                            for g in range(4):
                                ins = nc.tensor.matmul(p_bank[n][:, g * P:g * P + P],
                                                       w["wide_wq"][:, (4 * n + g) * P:(4 * n + g + 1) * P],
                                                       x_t[:], start=True, stop=True)
                            ins.then_inc(projected, 1)
                        pe.wait_ge(mask_used, s.at(1, 1))
                        for n in range(2):
                            pe.wait_ge(qk_taken, s.at(4, 1 + n))
                            for g in range(4):
                                ins = nc.tensor.matmul(p_bank[n][:, g * P:g * P + P],
                                                       w["wide_wk"][:, (4 * n + g) * P:(4 * n + g + 1) * P],
                                                       ctx_m[s.parity][:], start=True, stop=True)
                            ins.then_inc(projected, 1)
                        for n in range(2):
                            pe.wait_ge(qk_taken, s.at(4, 3 + n))
                            nc.tensor.matmul(p_bank[n][:], ctx_m[s.parity][:], w["wide_wv"][:, n * 512:n * 512 + 512],
                                             start=True, stop=True).then_inc(projected, 1)
                    if two.inside(TILES):
                        for n in range(2):
                            pe.wait_ge(normed, two.at(2, 1 + n))
                            if n == 0:
                                pe.wait_ge(pt_taken, two.at(2, 1))
                            elif s.inside(TILES):
                                pe.wait_ge(xt_taken, s.at(1, 1))
                            else:
                                pe.wait_ge(pt_taken, two.at(2, 2))
                            for g in range(4):
                                f = 4 * n + g
                                ins = nc.tensor.transpose(t_bank[1 - n][:, g * P:g * P + P],
                                                          heads_out[:, 2 * f:2 * f + 2, :].rearrange("p h d -> p (h d)"),
                                                          w["ident"][:])
                            ins.then_inc(ht_made, 1)
                    if one.inside(TILES):
                        pe.wait_ge(masked, one.at(1, 1))
                        for n in range(2):
                            if two.inside(TILES):
                                pe.wait_ge(ht_taken, two.at(2, 1 + n))
                            elif n == 1 and s.inside(TILES):
                                pe.wait_ge(xt_taken, s.at(1, 1))
                            for g in range(4):
                                f = 4 * n + g
                                ins = nc.tensor.transpose(t_bank[1 - n][:, g * P:g * P + P],
                                                          probs[:, 2 * f:2 * f + 2, :].rearrange("p h k -> p (h k)"),
                                                          w["ident"][:])
                            ins.then_inc(pt_made, 1)
                    if two.inside(TILES):
                        pe.wait_ge(ht_taken, two.at(2, 2))
                        for g in range(groups):
                            ins = nc.tensor.matmul(o_bank[0][:, 0:P], heads_t[:, g, :], w["wide_wo"][:, g, :],
                                                   start=(g == 0), stop=(g == groups - 1))
                        ins.then_inc(made_y, 1)
                    if s.inside(TILES):
                        pe.wait_ge(qk_taken, s.at(4, 4))
                        if s.past(1):
                            pe.wait_ge(shifted, s.at(2, 0))
                        for n in range(2):
                            for g in range(4):
                                for b in range(2):
                                    ins = nc.tensor.matmul(
                                        s_bank[n][SEQ * b:SEQ * b + SEQ, g * P:g * P + P],
                                        q_t[:, 4 * n + g, SEQ * b:SEQ * b + SEQ],
                                        k_bd[:, b, 4 * n + g].rearrange("p h k -> p (h k)"), start=True, stop=True)
                            ins.then_inc(scored, 1)
                    if one.inside(TILES):
                        pe.wait_ge(pt_taken, one.at(2, 2))
                        pe.wait_ge(v_taken, one.at(2, 2))
                        if two.inside(TILES):
                            pe.wait_ge(added, two.at(1, 1))
                        for n in range(2):
                            for g in range(4):
                                for b in range(2):
                                    ins = nc.tensor.matmul(
                                        o_bank[n][SEQ * b:SEQ * b + SEQ, g * P:g * P + P],
                                        probs_t[:, 4 * n + g, SEQ * b:SEQ * b + SEQ],
                                        v_bd[one.parity][:, b, 4 * n + g].rearrange("p h d -> p (h d)"),
                                        start=True, stop=True)
                            ins.then_inc(headed, 1)
                pipelined(pe, TILES, 2, body)


def narrow_attention(core, name, over_keys, masked_keys, keys_first=False):
    nc, w = core.nc, core.w
    hd = D // HEADS
    scale = hd ** -0.5
    with ExitStack() as stack:
        sb = lambda n, shape: core.sb(f"{name}_{n}", shape, stack=stack)
        sem = lambda n: core.stage_sem(f"{name}_{n}")
        xhat = [sb(f"xhat{n}", [P, P]) for n in range(2)]
        x_t = sb("x_t", [P, P])
        context = [sb(f"context{n}", [P, 2, 2 if over_keys else 1, SEQ]) for n in range(2)]
        row_t = sb("row_t", [P, P])
        col_t = sb("col_t", [P, P])
        col_bd = sb("col_bd", [P, 2, HEADS, SEQ])
        probs = [sb(f"probs{n}", [P, HEADS, SEQ]) for n in range(2)]
        top = sb("top", [P, HEADS])
        v_bd = [sb(f"v_bd{n}", [P, PAIRS, 2, 2, hd]) for n in range(2)]
        heads_t = sb("heads_t", [P, 2, P])
        rows_w = sb("rows_w", [P, 2, 2, P] if over_keys else [P, 2, 2, 2, P])
        based = [sb(f"based{n}", [P, P]) for n in range(2)]
        constant = sb("constant", [P, P])
        if over_keys:
            probs_t = sb("probs_t", [P, PAIRS, P])
            inverse_t = sb("inverse_t", [P, 2, P])
        else:
            total = sb("total", [P, HEADS])
            inverse = sb("inverse", [P, HEADS])
            v_biased = [sb(f"v_biased{n}", [P, P]) for n in range(2)]

        zeroed, weighted, const_made, const_ready = sem("zeroed"), sem("weighted"), sem("const_made"), sem("const_ready")
        staged, base_ready = sem("staged"), sem("base_ready")
        xhat_ready, xt_made, xt_taken = sem("xhat_ready"), sem("xt_made"), sem("xt_taken")
        projected, qk_taken = sem("projected"), sem("qk_taken")
        spread_a, spread_b = sem("spread_a"), sem("spread_b")
        v_made, v_taken = sem("v_made"), sem("v_taken")
        scored, masked, top_ready, shifted, exped = sem("scored"), sem("masked"), sem("top_ready"), sem("shifted"), sem("exped")
        pt_made, pt_taken = sem("pt_made"), sem("pt_taken")
        headed, ht_ready = sem("headed"), sem("ht_ready")
        inverted, summed, scaled = sem("inverted"), sem("summed"), sem("scaled")
        made_y, y_free, added = sem("made_y"), sem("y_free"), sem("added")

        q_bank = core.bank[0]
        v_bank = core.bank[1]
        s_bank = core.bank[2:4]
        pt_bank = core.bank[4:6]
        h_bank = core.bank[6]
        y_bank = core.bank[7]
        row_w, col_w = (name + "_wq", name + "_wk") if over_keys else (name + "_wk", name + "_wq")
        row_b, col_b = (name + "_bq", name + "_bk") if over_keys else (name + "_bk", name + "_bq")
        spread = lambda b: (col_bd[:, b], col_t[:, SEQ * b:SEQ * b + SEQ].unsqueeze(1).to_broadcast([P, HEADS, SEQ]),
                            w["head_mask"][:].unsqueeze(2).to_broadcast([P, HEADS, SEQ]))

        with nc.Block() as block:

            @block.gpsimd
            def _(pool):
                nc.gpsimd.memset(v_bd[0][:], 0.0)
                nc.gpsimd.memset(v_bd[1][:], 0.0).then_inc(zeroed, 1)
                arrived(core, pool, "ctx", "const")
                pool.wait_ge(const_ready, 1)

                def body(s):
                    if s.inside(TILES):
                        if s.past(2):
                            pool.wait_ge(v_made, s.at(1, -1))
                        tile = tile_of(w["ctx_t"], s).rearrange("p (b k) -> p b k", b=2)
                        for twice in range(2 if over_keys else 1):
                            ins = nc.gpsimd.tensor_copy(context[s.parity][:, :, twice, :], tile)
                        ins.then_inc(staged, 1)
                        pool.wait_ge(qk_taken, s.at(2, 2))
                        nc.gpsimd.tensor_tensor(*spread(1), ALU.mult).then_inc(spread_b, 1)
                    u = s.minus(2)
                    if u.inside(TILES):
                        if not over_keys:
                            pool.wait_ge(inverted, u.at(1, 1))
                            for b in range(2):
                                rows = slice(SEQ * b, SEQ * b + SEQ)
                                if b == 1:
                                    pool.wait_ge(scaled, u.at(2, 1))
                                elif s.inside(TILES):
                                    pool.wait_ge(spread_b, s.at(1, 1))
                                nc.gpsimd.tensor_tensor(
                                    v_bd[u.parity][rows, :, b],
                                    v_biased[u.parity][rows].rearrange("p (hp h d) -> p hp h d", h=2, d=hd),
                                    inverse[rows].rearrange("p (hp h) -> p hp h", h=2).unsqueeze(3)
                                    .to_broadcast([SEQ, PAIRS, 2, hd]), ALU.mult).then_inc(scaled, 1)
                            pool.wait_ge(scaled, u.at(2, 2))
                    u = s.minus(3)
                    if u.inside(TILES):
                        if u.past(2):
                            pool.wait_ge(added, u.at(1, -1))
                        nc.gpsimd.tensor_tensor(based[u.parity][:], tile_of(core.x, u), constant[:], ALU.add
                                                ).then_inc(base_ready, 1)
                pipelined(pool, TILES, 3, body)

            @block.vector
            def _(dve):
                arrived(core, dve, "const", name)
                dve.sem_inc(y_free, 1)
                for g in range(2):
                    for b in range(2):
                        for x in range(1 if over_keys else 2):
                            out = rows_w[:, g, b] if over_keys else rows_w[:, g, x, b]
                            mask = w["batch_mask"][:, b:b + 1] if over_keys else w["block_mask"][:, 2 * x + b:2 * x + b + 1]
                            ins = nc.vector.tensor_scalar(out, w[name + "_wo"][:, g], mask, None, ALU.mult)
                ins.then_inc(weighted, 1)
                if name == "attn3":
                    dve.wait_ge(const_made, 1)
                    nc.vector.tensor_tensor(constant[:], y_bank[:, 0:P], w["attn3_bo"][:], ALU.add).then_inc(const_ready, 1)
                else:
                    nc.vector.tensor_copy(constant[:], w[name + "_bo"][:]).then_inc(const_ready, 1)
                dve.wait_ge(zeroed, 1)

                def body(s):
                    if s.inside(TILES):
                        if s.past(2):
                            dve.wait_ge(xt_made, s.at(1, -1))
                        normalize(core, s, xhat[s.parity][:], core.rstd, xhat_ready)
                    u = s.minus(3)
                    if u.inside(TILES) and over_keys:
                        dve.wait_ge(headed, u.at(1, 1))
                        flat = "p g t -> p (g t)"
                        nc.vector.reciprocal(inverse_t[:].rearrange(flat), h_bank[:, 256:512]).then_inc(inverted, 1)
                        dve.wait_ge(inverted, u.at(1, 1))
                        nc.vector.tensor_tensor(heads_t[:].rearrange(flat), h_bank[:, 0:256],
                                                inverse_t[:].rearrange(flat), ALU.mult).then_inc(ht_ready, 1)
                    u = s.minus(2)
                    if u.inside(TILES) and not over_keys:
                        dve.wait_ge(exped, u.at(1, 1))
                        nc.vector.tensor_reduce(total[:], probs[u.parity][:], AX, ALU.add).then_inc(summed, 1)
                        dve.wait_ge(summed, u.at(1, 1))
                        if u.past(1):
                            dve.wait_ge(scaled, u.at(2, 0))
                        nc.vector.reciprocal(inverse[:], total[:]).then_inc(inverted, 1)
                    u = s.minus(1)
                    if u.inside(TILES):
                        for half in range(2):
                            h = slice(8 * half, 8 * half + 8)
                            s_ps = s_bank[half][:].rearrange("p (h k) -> p h k", k=SEQ)
                            dve.wait_ge(scored, u.at(2, 1 + half))
                            if masked_keys:
                                keys = tile_of(w["minus_huge"], u).unsqueeze(1).to_broadcast([P, 8, SEQ])
                                nc.vector.tensor_tensor(probs[u.parity][:, h], s_ps, keys, ALU.add).then_inc(masked, 1)
                            else:
                                nc.vector.tensor_reduce(top[:, h], s_ps, AX, ALU.max).then_inc(top_ready, 1)
                        if masked_keys:
                            dve.wait_ge(masked, u.at(2, 2))
                            nc.vector.tensor_reduce(top[:], probs[u.parity][:], AX, ALU.max).then_inc(top_ready, 2)
                        dve.wait_ge(top_ready, u.at(2, 2))
                        if masked_keys:
                            nc.vector.tensor_tensor(probs[u.parity][:], probs[u.parity][:],
                                                    top[:].unsqueeze(2).to_broadcast([P, HEADS, SEQ]), ALU.subtract
                                                    ).then_inc(shifted, 1)
                        else:
                            for half in range(2):
                                h = slice(8 * half, 8 * half + 8)
                                ins = nc.vector.tensor_tensor(
                                    probs[u.parity][:, h], s_bank[half][:].rearrange("p (h k) -> p h k", k=SEQ),
                                    top[:, h].unsqueeze(2).to_broadcast([P, 8, SEQ]), ALU.subtract)
                            ins.then_inc(shifted, 1)
                        dve.wait_ge(v_made, u.at(1, 1))
                        if over_keys:
                            v = v_bank[:, 0:256].rearrange("p (b hp h d) -> p b hp h d", b=2, hp=PAIRS, h=2)
                            for h2 in range(2):
                                rows = slice(SEQ * h2, SEQ * h2 + SEQ)
                                ins = nc.vector.tensor_copy(
                                    v_bd[u.parity][rows, :, :, h2, :].rearrange("p hp b d -> p b hp d"), v[rows, :, :, h2, :])
                            ins.then_inc(v_taken, 1)
                        else:
                            if u.past(2):
                                dve.wait_ge(scaled, u.at(2, -2))
                            nc.vector.tensor_tensor(v_biased[u.parity][:], v_bank[:, 0:P], w[name + "_bv"][:], ALU.add
                                                    ).then_inc(v_taken, 1)
                    if s.inside(TILES):
                        dve.wait_ge(qk_taken, s.at(2, 2))
                        nc.vector.tensor_tensor(*spread(0), ALU.mult).then_inc(spread_a, 1)
                    u = s.minus(3)
                    if u.inside(TILES):
                        dve.wait_ge(made_y, u.at(1, 1))
                        dve.wait_ge(base_ready, u.at(1, 1))
                        x_u = tile_of(core.x, u)
                        nc.vector.tensor_tensor(x_u, y_bank[:, 0:P], based[u.parity][:], ALU.add).then_inc(added, 1)
                        token_stats(core, dve, added, u)
                pipelined(dve, TILES, 3, body)

            @block.scalar
            def _(act):
                arrived(core, act, name)

                def body(s):
                    if s.inside(TILES):
                        act.wait_ge(xt_made, s.at(1, 1))
                        nc.scalar.copy(x_t[:], q_bank[:, 0:P]).then_inc(xt_taken, 1)
                        act.wait_ge(projected, s.at(1, 1))
                        nc.scalar.activation(row_t[:], q_bank[:, P:2 * P], ACT.Identity, bias=w[row_b][:, 0:1]
                                             ).then_inc(qk_taken, 1)
                        nc.scalar.activation(col_t[:], q_bank[:, 2 * P:3 * P], ACT.Identity, bias=w[col_b][:, 0:1]
                                             ).then_inc(qk_taken, 1)
                    u = s.minus(2)
                    if u.inside(TILES) and over_keys:
                        for n in range(2):
                            act.wait_ge(pt_made, u.at(2, 1 + n))
                            nc.scalar.copy(probs_t[:, 4 * n:4 * n + 4, :].rearrange("p g t -> p (g t)"), pt_bank[n][:]
                                           ).then_inc(pt_taken, 1)
                    u = s.minus(3)
                    if u.inside(TILES) and not over_keys:
                        act.wait_ge(headed, u.at(1, 1))
                        nc.scalar.copy(heads_t[:].rearrange("p g t -> p (g t)"), h_bank[:, 0:256]).then_inc(ht_ready, 1)
                    u = s.minus(1)
                    if u.inside(TILES):
                        act.wait_ge(shifted, u.at(1, 1))
                        nc.scalar.activation(probs[u.parity][:], probs[u.parity][:], ACT.Exp, scale=scale).then_inc(exped, 1)
                pipelined(act, TILES, 3, body)

            @block.tensor
            def _(pe):
                arrived(core, pe, "ctx", "const", name)
                if name == "attn3":
                    pe.wait_ge(weighted, 1)
                    nc.tensor.matmul(y_bank[:, 0:P], w["attn3_bv"][:], w["attn3_wo_plain"][:], start=True, stop=True
                                     ).then_inc(const_made, 1)
                pe.wait_ge(weighted, 1)
                pe.wait_ge(const_ready, 1)

                def body(s):
                    u = s.minus(1)
                    if u.inside(TILES):
                        pe.wait_ge(spread_a, u.at(1, 1))
                        pe.wait_ge(spread_b, u.at(1, 1))
                        if u.past(1):
                            pe.wait_ge(shifted, u.at(1, 0))
                        for n in range(2):
                            for b in range(2):
                                ins = nc.tensor.matmul(
                                    s_bank[n][SEQ * b:SEQ * b + SEQ, :], row_t[:, SEQ * b:SEQ * b + SEQ],
                                    col_bd[:, b, 8 * n:8 * n + 8].rearrange("p h k -> p (h k)"), start=True, stop=True)
                            ins.then_inc(scored, 1)
                    if s.inside(TILES):
                        pe.wait_ge(xhat_ready, s.at(1, 1))
                        if s.past(1):
                            pe.wait_ge(qk_taken, s.at(2, 0))
                        nc.tensor.transpose(q_bank[:, 0:P], xhat[s.parity][:], w["ident"][:]).then_inc(xt_made, 1)
                    u = s.minus(1)
                    if u.inside(TILES):
                        if u.past(1):
                            pe.wait_ge(v_taken, u.at(1, 0))
                        if over_keys:
                            for b in range(2):
                                ins = nc.tensor.matmul(v_bank[:, b * P:b * P + P],
                                                       context[u.parity][:, b].rearrange("p t k -> p (t k)"),
                                                       w[name + "_wv"][:], start=True, stop=True)
                        else:
                            ins = nc.tensor.matmul(v_bank[:, 0:P], context[u.parity][:].rearrange("p b t k -> p (b t k)"),
                                                   w[name + "_wv"][:],
                                                   start=True, stop=True)
                        ins.then_inc(v_made, 1)
                    if s.inside(TILES):
                        pe.wait_ge(xt_taken, s.at(1, 1))
                        pe.wait_ge(staged, s.at(1, 1))
                        ctx_rhs = context[s.parity][:, :, 0]
                        rows, cols = (x_t[:], ctx_rhs) if over_keys else (ctx_rhs, x_t[:])
                        nc.tensor.matmul(q_bank[:, P:2 * P], w[row_w][:], rows, start=True, stop=True)
                        nc.tensor.matmul(q_bank[:, 2 * P:3 * P], w[col_w][:], cols, start=True, stop=True
                                         ).then_inc(projected, 1)
                    u = s.minus(2)
                    if u.inside(TILES) and over_keys:
                        pe.wait_ge(exped, u.at(1, 1))
                        for n in range(2):
                            if u.past(1):
                                pe.wait_ge(pt_taken, u.at(2, -1 + n))
                            for g in range(4):
                                f = 4 * n + g
                                ins = nc.tensor.transpose(
                                    pt_bank[n][:, g * P:g * P + P],
                                    probs[u.parity][:, 2 * f:2 * f + 2, :].rearrange("p h k -> p (h k)"), w["ident"][:])
                            ins.then_inc(pt_made, 1)
                    u = s.minus(3)
                    if u.inside(TILES):
                        pe.wait_ge(ht_ready, u.at(1, 1))
                        pe.wait_ge(y_free, 1)
                        if u.past(1):
                            pe.wait_ge(added, u.at(1, 0))
                        terms = [(g, x) for g in range(2) for x in range(1 if over_keys else 2)]
                        for n, (g, x) in enumerate(terms):
                            for b in range(2):
                                at = SEQ * (b if over_keys else x)
                                ins = nc.tensor.matmul(
                                    y_bank[SEQ * b:SEQ * b + SEQ, 0:P], heads_t[:, g, at:at + SEQ],
                                    rows_w[:, g, b] if over_keys else rows_w[:, g, x, b],
                                    start=(n == 0), stop=(n == len(terms) - 1))
                        ins.then_inc(made_y, 1)
                    u = s.minus(2)
                    if u.inside(TILES):
                        if over_keys:
                            pe.wait_ge(pt_taken, u.at(2, 2))
                        else:
                            pe.wait_ge(scaled, u.at(2, 2))
                        for g in range(2):
                            for j in range(4):
                                hp = 4 * g + j
                                rhs = probs_t[:, hp, :] if over_keys else \
                                    probs[u.parity][:, 2 * hp:2 * hp + 2, :].rearrange("p h l -> p (h l)")
                                ins = nc.tensor.matmul(
                                    h_bank[32 * j:32 * j + 32, g * P:g * P + P],
                                    v_bd[u.parity][:, hp].rearrange("p b h d -> p (b h d)"), rhs, start=True, stop=True)
                        if over_keys:
                            for g in range(2):
                                for j in range(4):
                                    ins = nc.tensor.matmul(h_bank[32 * j:32 * j + 32, (2 + g) * P:(3 + g) * P],
                                                           w["half_ones"][:], probs_t[:, 4 * g + j, :], start=True, stop=True)
                        ins.then_inc(headed, 1)
                pipelined(pe, TILES, 3, body)


def prepare_mask(core):
    nc, w = core.nc, core.w
    with nc.Block() as block:

        @block.vector
        def _(dve):
            arrived(core, dve, "mask_i")
            nc.vector.tensor_scalar(w["minus_huge"][:], w["mask_i_keys"][:], 0.0, MASKED, ALU.is_gt, ALU.mult)


def unit_of(buffer, u):
    at = u.at(UNIT, 0)
    span = slice(at, at + UNIT) if isinstance(at, int) else bass.ds(at, UNIT)
    return buffer[:, span, :].rearrange("p a c -> p (a c)")


def units(eng, body):
    with eng.Fori(0, UNITS) as i:
        body(Step(i, 0, 1))


def units_ahead(eng, ahead, body):
    ahead(Step(None, 0))
    with eng.Fori(0, UNITS - 1) as i:
        u = Step(i, 0, 1)
        body(u, lambda: ahead(u.minus(-1)))
    body(Step(None, UNITS - 1), lambda: None)


def quantize(core, eng, done, count, value, parts, out):
    nc = core.nc
    power, rounded = parts
    nc.vector.tensor_scalar(power.bitcast(U32), value.bitcast(U32), 0x7F800000, None, ALU.bitwise_and).then_inc(done, 1)
    eng.wait_ge(done, count(1))
    nc.vector.tensor_scalar(power, power, 2.0 ** -6, 1.5 * 2.0 ** 20, ALU.max, ALU.mult).then_inc(done, 1)
    eng.wait_ge(done, count(2))
    nc.vector.tensor_tensor(rounded, value, power, ALU.add).then_inc(done, 1)
    eng.wait_ge(done, count(3))
    nc.vector.tensor_tensor(rounded, rounded, power, ALU.subtract).then_inc(done, 1)
    eng.wait_ge(done, count(4))
    nc.vector.tensor_scalar(power, rounded, 2.0 ** 64 / 470 * 2.0 ** 64, 0.0, ALU.mult, ALU.mult).then_inc(done, 1)
    eng.wait_ge(done, count(5))
    nc.vector.tensor_tensor(out, rounded, power, ALU.add).then_inc(done, 1)


QUANTIZE_STEPS = 6


def fp8_product(core):
    nc, w = core.nc, core.w
    with ExitStack() as stack:
        sb = lambda n, shape, dt=F32: core.sb("fp8_" + n, shape, dt, stack)
        sem = lambda n: core.stage_sem("fp8_" + n)
        x_bf = sb("x_bf", [P, UNIT, P], BF16)
        value, power, rounded = (sb(n, [P, UTOK]) for n in ("value", "power", "rounded"))
        x_q = sb("x_q", [P, UTOK], BF16)
        x_qt = sb("x_qt", [P, UTOK], BF16)
        kernel_q = sb("kernel_q", [P, P], BF16)
        ident_bf = sb("ident_bf", [P, P], BF16)
        inverses = sb("inverses", [P, 2])
        product = sb("product", [P, 1])
        y_bf, y_biased = sb("y_bf", [P, UTOK], BF16), sb("y_biased", [P, UTOK], BF16)

        prepared, k_rounding, normed = sem("prepared"), sem("k_rounding"), sem("normed")
        rounding, xt_made, xt_taken = sem("rounding"), sem("xt_made"), sem("xt_taken")
        made_y, y_cast, y_summed, added = sem("made_y"), sem("y_cast"), sem("y_summed"), sem("added")
        t_bank, y_bank = core.bank[0], core.bank[1]
        t_bf = t_bank[:].bitcast(BF16)[:, 0:UTOK]

        with nc.Block() as block:

            @block.vector
            def _(dve):
                arrived(core, dve, "fp8", "ctx")
                nc.vector.tensor_copy(ident_bf[:], w["ident"][:])
                nc.vector.tensor_tensor(product[:], w["fp8_scales"][:, 0:1], w["fp8_scales"][:, 1:2], ALU.mult)
                nc.vector.reciprocal(inverses[:], w["fp8_scales"][:]).then_inc(prepared, 1)
                dve.wait_ge(prepared, 1)
                nc.vector.tensor_scalar(value[:, 0:P], w["fp8_kernel"][:], inverses[:, 1:2], None, ALU.mult).then_inc(prepared, 1)
                dve.wait_ge(prepared, 2)
                dve.sem_inc(y_cast, 1)
                quantize(core, dve, k_rounding, lambda n: n, value[:, 0:P], (power[:, 0:P], rounded[:, 0:P]), kernel_q[:])
                dve.wait_ge(k_rounding, QUANTIZE_STEPS)

                def ahead(u):
                    for t in range(UNIT):
                        normalize(core, u, x_bf[:, t], core.rstd, normed if t == UNIT - 1 else None, UNIT, t)
                    dve.wait_ge(normed, u.at(2, 1))
                    nc.vector.tensor_scalar(value[:], x_bf[:].rearrange("p t c -> p (t c)"), inverses[:, 0:1], None, ALU.mult
                                            ).then_inc(normed, 1)
                    dve.wait_ge(normed, u.at(2, 2))
                    if u.i is not None or u.off:
                        dve.wait_ge(xt_made, u.at(1, 0))
                    quantize(core, dve, rounding, lambda n: u.at(QUANTIZE_STEPS, n), value[:], (power[:], rounded[:]), x_q[:])

                def body(u, then):
                    then()
                    dve.wait_ge(made_y, u.at(1, 1))
                    nc.vector.tensor_scalar(y_bf[:], y_bank[:], product[:, 0:1], None, ALU.mult).then_inc(y_cast, 1)
                    dve.wait_ge(y_cast, u.at(1, 2))
                    nc.vector.tensor_tensor(y_biased[:].rearrange("p (t c) -> p t c", t=UNIT),
                                            y_bf[:].rearrange("p (t c) -> p t c", t=UNIT),
                                            w["fp8_bias"][:].unsqueeze(1).to_broadcast([P, UNIT, P]), ALU.add).then_inc(y_summed, 1)
                    dve.wait_ge(y_summed, u.at(1, 1))
                    nc.vector.tensor_tensor(unit_of(core.x, u), unit_of(core.x, u), y_biased[:], ALU.add).then_inc(added, 1)
                    unit_stats(core, dve, added, u)
                units_ahead(dve, ahead, body)

            @block.scalar
            def _(act):
                def body(u):
                    act.wait_ge(xt_made, u.at(1, 1))
                    nc.scalar.copy(x_qt[:], t_bf).then_inc(xt_taken, 1)
                units(act, body)

            @block.tensor
            def _(pe):
                pe.wait_ge(k_rounding, QUANTIZE_STEPS)

                def body(u):
                    pe.wait_ge(rounding, u.at(QUANTIZE_STEPS, QUANTIZE_STEPS))
                    for t in range(UNIT):
                        ins = nc.tensor.transpose(t_bf[:, t * P:t * P + P], x_q[:, t * P:t * P + P], ident_bf[:])
                    ins.then_inc(xt_made, 1)
                    pe.wait_ge(xt_taken, u.at(1, 1))
                    pe.wait_ge(y_cast, u.at(1, 1))
                    for t in range(UNIT):
                        ins = nc.tensor.matmul(y_bank[:, t * P:t * P + P], x_qt[:, t * P:t * P + P], kernel_q[:],
                                               start=True, stop=True)
                    ins.then_inc(made_y, 1)
                units(pe, body)


def unit_stats(core, dve, added, u):
    dve.wait_ge(added, u.at(1, 1))
    dve.wait_ge(added, 1)
    for t in range(UNIT):
        core.nc.vector.bn_stats(tile_of(core.stats, u, UNIT, t), tile_of(core.x, u, UNIT, t))


def experts(core, name, prefetch=()):
    nc, w = core.nc, core.w
    gated = name == "moe3"
    deep = name == "moe0"
    biased = not gated
    n_exp = EXPERTS + gated
    nf = 2 if gated else 4
    act_fn = {"moe0": ACT.Relu, "moe2": ACT.Gelu, "moe3": ACT.Silu}[name]
    RING = 4
    router_uses = 8 if deep else 0
    uses = router_uses + (0 if gated else n_exp * nf)
    steps = 2 * n_exp
    flat = "p t e -> p (t e)"
    with ExitStack() as stack:
        sb = lambda n, shape, dt=F32: core.sb(f"{name}_{n}", shape, dt, stack)
        sem = lambda n: core.stage_sem(f"{name}_{n}")
        xhat = sb("xhat", [P, UNIT, P])
        x_t = sb("x_t", [P, UTOK])
        hidden = [sb(f"hidden{n}", [P, nf, UTOK]) for n in range(2)]
        if deep:
            router1, router2 = sb("router1", [P, 4, UTOK]), sb("router2", [P, 4, UTOK])
        if gated:
            gate = [sb(f"gate{n}", [P, UTOK]) for n in range(2)]
        logits_t = sb("logits_t", [EXPERTS, UTOK])
        score = sb("score", [P, UNIT, EXPERTS])
        best = sb("best", [P, UNIT, 8])
        index = sb("index", [P, UNIT, 8], U32)
        index_f = sb("index_f", [P, UNIT, 2])
        one_hot = sb("one_hot", [P, UNIT, 2, EXPERTS])
        chosen = sb("chosen", [P, UNIT, EXPERTS])
        weight = sb("weight", [P, UNIT, EXPERTS])
        row = sb("row", [P, UNIT])
        row_inv = sb("row_inv", [P, UNIT])
        pair_weight = sb("pair_weight", [P, UNIT, 2])
        weight_t = sb("weight_t", [EXPERTS, UTOK])

        xhat_ready, transposed, xt_taken = sem("xhat_ready"), sem("transposed"), sem("xt_taken")
        hid_made, hid_taken = sem("hid_made"), sem("hid_taken")
        gate_made, up_made, gated_ready, h_ready = sem("gate_made"), sem("up_made"), sem("gated"), sem("h_ready")
        lt_made, lt_taken, logits_made = sem("lt_made"), sem("lt_taken"), sem("logits_made")
        route, squashed = sem("route"), sem("squashed")
        settled = sem("settled")
        placed, weighted_t, wt_taken, bias_made = sem("placed"), sem("weights_t"), sem("wt_taken"), sem("bias_made")
        y_made, y_taken, added = sem("y_made"), sem("y_taken"), sem("added")

        t_bank, small, y_banks = core.bank[6], core.bank[7], core.bank[4:6]
        CHAIN = 12 if deep else 11

        with nc.Block() as block:

            @block.sync
            def _(sp):
                start_loads(core, sp, prefetch)

            @block.vector
            def _(dve):
                arrived(core, dve, "ctx", name, "moe_const")
                dve.sem_inc(y_taken, 2)
                if gated:
                    dve.sem_inc(h_ready, 2)

                def ahead(u):
                    dve.wait_ge(transposed, u.at(1, 1))
                    for t in range(UNIT):
                        normalize(core, u, xhat[:, t], core.rstd, xhat_ready if t == UNIT - 1 else None, UNIT, t)

                def routing(u):
                    n = [0]

                    def link(ins):
                        n[0] += 1
                        ins.then_inc(route, 1)
                        dve.wait_ge(route, u.at(CHAIN, n[0]))

                    logits = small[:, 0:UNIT * EXPERTS].rearrange("p (t e) -> p t e", t=UNIT)
                    wide = lambda v: v.unsqueeze(2).to_broadcast([P, UNIT, EXPERTS])
                    dve.wait_ge(logits_made, u.at(1, 1))
                    if deep:
                        link(nc.vector.tensor_reduce(row[:], logits, AX, ALU.max))
                        link(nc.vector.tensor_tensor(score[:], logits, wide(row[:]), ALU.subtract))
                        dve.wait_ge(squashed, u.at(1, 1))
                        link(nc.vector.tensor_reduce(row[:], score[:], AX, ALU.add))
                        link(nc.vector.reciprocal(row_inv[:], row[:]))
                        link(nc.vector.tensor_tensor(score[:], score[:], wide(row_inv[:]), ALU.mult))
                    else:
                        link(nc.vector.tensor_copy(score[:], logits))
                    dve.sem_inc(settled, 1)
                    for t in range(UNIT):
                        ins = nc.vector.max(best[:, t], score[:, t])
                    link(ins)
                    dve.sem_inc(settled, 1)
                    for t in range(UNIT):
                        ins = nc.vector.max_index(index[:, t], best[:, t], score[:, t])
                    link(ins)
                    link(nc.vector.tensor_copy(index_f[:], index[:, :, 0:2]))
                    link(nc.vector.tensor_tensor(
                        one_hot[:], w["numbers"][:].unsqueeze(1).unsqueeze(1).to_broadcast([P, UNIT, 2, EXPERTS]),
                        index_f[:].unsqueeze(3).to_broadcast([P, UNIT, 2, EXPERTS]), ALU.is_equal))
                    if deep:
                        link(nc.vector.tensor_tensor(chosen[:], one_hot[:, :, 0], one_hot[:, :, 1], ALU.add))
                        dve.wait_ge(placed, u.at(1, 1))
                        link(nc.vector.scalar_tensor_tensor(
                            chosen[:].rearrange(flat), small[:, 0:UNIT * EXPERTS], float(CAPACITY),
                            chosen[:].rearrange(flat), ALU.is_lt, ALU.mult))
                        link(nc.vector.tensor_tensor(weight[:], chosen[:], score[:], ALU.mult))
                    else:
                        link(nc.vector.tensor_tensor(row[:], best[:, :, 1], best[:, :, 0], ALU.subtract))
                        dve.wait_ge(squashed, u.at(1, 1))
                        link(nc.vector.tensor_scalar(pair_weight[:, :, 0], row_inv[:], -0.5, 0.5, ALU.mult, ALU.add))
                        link(nc.vector.tensor_scalar(pair_weight[:, :, 1], row_inv[:], 0.5, 0.5, ALU.mult, ALU.add))
                        link(nc.vector.tensor_tensor(chosen[:], one_hot[:, :, 0], wide(pair_weight[:, :, 0]), ALU.mult))
                        link(nc.vector.tensor_tensor(score[:], one_hot[:, :, 1], wide(pair_weight[:, :, 1]), ALU.mult))
                        link(nc.vector.tensor_tensor(weight[:], chosen[:], score[:], ALU.add))
                    assert n[0] == CHAIN
                    if biased:
                        dve.wait_ge(weighted_t, u.at(1, 1))
                        nc.vector.tensor_copy(weight_t[:], small[0:EXPERTS, :]).then_inc(wt_taken, 1)
                        dve.wait_ge(bias_made, u.at(1, 1))
                        nc.vector.tensor_tensor(unit_of(core.x, u), small[:], unit_of(core.x, u), ALU.add).then_inc(wt_taken, 1)
                        dve.wait_ge(wt_taken, u.at(2, 2))

                def half_gated(u, e, f):
                    dve.wait_ge(gated_ready, u.at(steps, 2 * e + f + 3))
                    dve.wait_ge(up_made, u.at(steps, 2 * e + f + 1))
                    nc.vector.tensor_tensor(hidden[e % 2][:, f], core.bank[2 + f][:], gate[f][:], ALU.mult).then_inc(h_ready, 1)

                def add(u, e):
                    dve.wait_ge(y_made, u.at(n_exp, e + 1))
                    if e or not biased:
                        dve.wait_ge(y_taken, u.at(n_exp, e + 2))
                    for t in range(UNIT):
                        x_u = tile_of(core.x, u, UNIT, t)
                        y = y_banks[e % 2][:, t * P:t * P + P]
                        if gated and e == 0:
                            ins = nc.vector.tensor_tensor(x_u, y, x_u, ALU.add)
                        else:
                            k = e - gated
                            ins = nc.vector.scalar_tensor_tensor(x_u, y, weight[:, t, k:k + 1], x_u, ALU.mult, ALU.add)
                    ins.then_inc(y_taken, 1)

                def body(u, then):
                    if gated:
                        for e in range(n_exp):
                            for f in range(nf):
                                half_gated(u, e, f)
                            if e == 1:
                                routing(u)
                            if e >= 1:
                                add(u, e - 1)
                            if e == 5:
                                then()
                        add(u, n_exp - 1)
                    else:
                        routing(u)
                        for e in range(n_exp):
                            add(u, e)
                            if e == 4:
                                then()
                    dve.wait_ge(y_taken, u.at(n_exp, n_exp + 2))
                    dve.wait_ge(y_taken, 1)
                    for t in range(UNIT):
                        nc.vector.bn_stats(tile_of(core.stats, u, UNIT, t), tile_of(core.x, u, UNIT, t))
                units_ahead(dve, ahead, body)

            @block.scalar
            def _(act):
                arrived(core, act, name)
                if gated:
                    act.sem_inc(gated_ready, 2)
                else:
                    act.sem_inc(hid_taken, RING)

                def take(u, j, out, func, bias):
                    act.wait_ge(hid_made, u.at(uses, j + 1))
                    nc.scalar.activation(out, core.bank[j % RING][:], func, bias=bias).then_inc(hid_taken, 1)

                def body(u):
                    act.wait_ge(transposed, u.at(1, 2))
                    nc.scalar.copy(x_t[:], t_bank[:]).then_inc(xt_taken, 1)
                    if deep:
                        for f in range(4):
                            take(u, f, router1[:, f], ACT.Relu, w["moe0_rb1"][:, f:f + 1])
                        for f in range(4):
                            take(u, 4 + f, router2[:, f], ACT.Relu, w["moe0_rb2"][:, f:f + 1])
                    act.wait_ge(lt_made, u.at(1, 1))
                    if name == "moe2":
                        nc.scalar.copy(logits_t[:], t_bank[0:EXPERTS, :]).then_inc(lt_taken, 1)
                    else:
                        nc.scalar.activation(logits_t[:], t_bank[0:EXPERTS, :], ACT.Identity, bias=w[name + "_rb"][:, 0:1]
                                             ).then_inc(lt_taken, 1)
                    for e in range(n_exp):
                        for f in range(nf):
                            if gated:
                                act.wait_ge(gate_made, u.at(steps, 2 * e + f + 1))
                                act.wait_ge(h_ready, u.at(steps, 2 * e + f + 1))
                                nc.scalar.activation(gate[f][:], core.bank[f][:], act_fn).then_inc(gated_ready, 1)
                            else:
                                take(u, router_uses + e * nf + f, hidden[e % 2][:, f], act_fn,
                                     w[name + "_b1"][:, e * nf + f:e * nf + f + 1])
                        if e == 1:
                            if deep:
                                act.wait_ge(route, u.at(CHAIN, 2))
                                nc.scalar.activation(score[:], score[:], ACT.Exp).then_inc(squashed, 1)
                            else:
                                act.wait_ge(route, u.at(CHAIN, 6))
                                nc.scalar.activation(row_inv[:], row[:], ACT.Tanh, scale=0.5).then_inc(squashed, 1)
                units(act, body)

            @block.tensor
            def _(pe):
                arrived(core, pe, "ctx", name, "moe_const")
                pe.sem_inc(transposed, 1)

                def ring(u, j, terms):
                    pe.wait_ge(hid_taken, u.at(uses, j + 1))
                    for n, (lhs, rhs) in enumerate(terms):
                        ins = nc.tensor.matmul(core.bank[j % RING][:], lhs, rhs, start=(n == 0), stop=(n == len(terms) - 1))
                    ins.then_inc(hid_made, 1)

                def hidden_layer(u, e):
                    for f in range(nf):
                        at = slice(f * P, f * P + P)
                        if gated:
                            pe.wait_ge(gated_ready, u.at(steps, 2 * e + f + 1))
                            nc.tensor.matmul(core.bank[f][:], w["moe3_w1"][:, e, at], x_t[:], start=True, stop=True
                                             ).then_inc(gate_made, 1)
                            pe.wait_ge(h_ready, u.at(steps, 2 * e + f + 1))
                            nc.tensor.matmul(core.bank[2 + f][:], w["moe3_w3"][:, e, at], x_t[:], start=True, stop=True
                                             ).then_inc(up_made, 1)
                        else:
                            ring(u, router_uses + e * nf + f, [(w[name + "_w1"][:, e, at], x_t[:])])

                def output(u, e):
                    pe.wait_ge(y_taken, u.at(n_exp, e + 1))
                    if gated:
                        pe.wait_ge(h_ready, u.at(steps, 2 * e + 4))
                    else:
                        pe.wait_ge(hid_taken, u.at(uses, router_uses + (e + 1) * nf + RING))
                    for t in range(UNIT):
                        for f in range(nf):
                            ins = nc.tensor.matmul(y_banks[e % 2][:, t * P:t * P + P], hidden[e % 2][:, f, t * P:t * P + P],
                                                   w[name + "_w2"][:, e, f], start=(f == 0), stop=(f == nf - 1))
                    ins.then_inc(y_made, 1)

                def route_logits(u):
                    pe.wait_ge(lt_taken, u.at(1, 1))
                    pe.sem_inc(settled, 1)
                    for t in range(UNIT):
                        ins = nc.tensor.transpose(small[:, t * EXPERTS:(t + 1) * EXPERTS], logits_t[:, t * P:t * P + P],
                                                  w["ident"][0:EXPERTS, 0:EXPERTS])
                    ins.then_inc(logits_made, 1)

                def route_places(u):
                    pe.wait_ge(route, u.at(CHAIN, CHAIN - 2))
                    nc.tensor.matmul(small[:, 0:UNIT * EXPERTS], w["earlier"][:], chosen[:].rearrange(flat),
                                     start=True, stop=True).then_inc(placed, 1)

                def route_weights(u):
                    pe.wait_ge(route, u.at(CHAIN, CHAIN))
                    for t in range(UNIT):
                        ins = nc.tensor.transpose(small[0:EXPERTS, t * P:t * P + P], weight[:, t], w["ident"][:])
                    ins.then_inc(weighted_t, 1)

                def route_bias(u):
                    pe.wait_ge(wt_taken, u.at(2, 1))
                    for t in range(UNIT):
                        ins = nc.tensor.matmul(small[:, t * P:t * P + P], weight_t[:, t * P:t * P + P], w[name + "_b2"][:],
                                               start=True, stop=True)
                    ins.then_inc(bias_made, 1)

                def body(u):
                    pe.wait_ge(xhat_ready, u.at(1, 1))
                    for t in range(UNIT):
                        ins = nc.tensor.transpose(t_bank[:, t * P:t * P + P], xhat[:, t], w["ident"][:])
                    ins.then_inc(transposed, 1)
                    pe.wait_ge(xt_taken, u.at(1, 1))
                    if deep:
                        for f in range(4):
                            ring(u, f, [(w["moe0_rw1"][:, f * P:f * P + P], x_t[:])])
                        for g in range(4):
                            pe.wait_ge(hid_taken, u.at(uses, 4 + RING))
                            ring(u, 4 + g, [(w["moe0_rw2"][:, f, g * P:g * P + P], router1[:, f]) for f in range(4)])
                        pe.wait_ge(hid_taken, u.at(uses, 8 + RING))
                        terms = [(w["moe0_rw"][:, f], router2[:, f]) for f in range(4)]
                    else:
                        terms = [(w[name + "_rw"][:], x_t[:])]
                    for n, (lhs, rhs) in enumerate(terms):
                        ins = nc.tensor.matmul(t_bank[0:EXPERTS, :], lhs, rhs, start=(n == 0), stop=(n == len(terms) - 1))
                    ins.then_inc(lt_made, 1)
                    for e in range(n_exp + 1):
                        if e < n_exp:
                            hidden_layer(u, e)
                        if e >= 1:
                            output(u, e - 1)
                        if e == 0:
                            route_logits(u)
                        if e == 1 and deep:
                            route_places(u)
                        if e == 2 and biased:
                            route_weights(u)
                            route_bias(u)
                units(pe, body)


def by_query(mask):
    rows = mask.reshape(TILES, 2, 1, SEQ).transpose(1, 2, 0, 3)
    return np.broadcast_to(rows, (2, SEQ, TILES, SEQ)).reshape(P, TILES, SEQ)


def twice_rows(weights):
    rows = weights.reshape(2, 4, 1, 16, -1).transpose(1, 2, 3, 0, 4)
    return np.broadcast_to(rows, (4, 2, 16, 2, rows.shape[-1])).reshape(P, 2, -1)


def by_group(weights):
    return weights.reshape(-1, P, weights.shape[-1]).transpose(1, 0, 2)


def outputs_of(weights):
    return weights.reshape(weights.shape[0], -1, P, weights.shape[-1]).transpose(2, 0, 1, 3)


def store(core, out):
    stored = core.sem("stored")
    with core.nc.Block() as block:

        @block.sync
        def _(sp):
            half = TILES // 2
            for q in range(2):
                sp.dma_start(out.rearrange("(t p) c -> p t c", p=P)[:, q * half:(q + 1) * half, :],
                             core.x[:, q * half:(q + 1) * half, :]).then_inc(stored, DMA_INC)
            sp.wait_ge(stored, 2 * DMA_INC)


def program(nc, args, out):
    with ExitStack() as stack:
        core = Core(nc, stack, args)
        resident = ["ctx", "const", "attn1", "moe0", "moe_const", "fp8", "attn2", "attn3", "mask_i"]
        allocate(core, resident)
        core.w["minus_huge"] = core.sb("minus_huge", [P, TILES, SEQ])
        with ExitStack() as early:
            allocate(core, ["wide"], early)
            load_and_first_stats(core, ["ctx", "wide"] + resident[1:])
            norm_scale(core, 0)
            wide_attention(core)
            core.end_of_stage()
        allocate(core, ["moe2", "moe3"])
        norm_scale(core, 1)
        experts(core, "moe0", prefetch=["moe2", "moe3"])
        core.end_of_stage()
        prepare_mask(core)
        norm_scale(core, 2)
        narrow_attention(core, "attn1", True, True)
        core.end_of_stage()
        norm_scale(core, 3)
        fp8_product(core)
        core.end_of_stage()
        norm_scale(core, 4)
        narrow_attention(core, "attn2", False, False)
        core.end_of_stage()
        norm_scale(core, 5)
        experts(core, "moe2")
        core.end_of_stage()
        norm_scale(core, 6)
        narrow_attention(core, "attn3", True, False)
        core.end_of_stage()
        norm_scale(core, 7)
        experts(core, "moe3")
        store(core, out)


def kernel(**inputs):
    import concourse.bacc as bacc
    from concourse.bass_utils import run_bass_kernel_spmd

    a = {name: np.asarray(value) for name, value in inputs.items()}
    laid = {}
    laid["x"] = a["x"].reshape(TOKENS, D)
    laid["ident"] = np.eye(P, dtype=np.float32)
    laid["ctx_t"] = a["ctx_1024"].reshape(TILES, P, D).transpose(2, 0, 1)
    mask_f = a["mask_BxS2_fk1"]
    laid["mask_f_rows"] = mask_f.reshape(TILES, P)
    laid["mask_f_col"] = mask_f.reshape(TILES, P).T
    laid["mask_f_keys"] = by_query(mask_f)
    laid["wide_wq"], laid["wide_wk"], laid["wide_wv"] = a["L0_xattn_Wq"], a["L0_xattn_Wk"], a["L0_xattn_Wv"]
    laid["wide_wo"] = a["L0_xattn_Wo"].reshape(8, P, D).transpose(1, 0, 2)

    heads, halves, batches = np.arange(P) // 8, np.arange(P) // SEQ, np.arange(P) // 16 % 2
    pair_half = np.arange(P) // 8 % 2
    laid["head_mask"] = (heads[:, None] == np.arange(HEADS)).astype(np.float32)
    laid["batch_mask"] = (batches[:, None] == np.arange(2)).astype(np.float32)
    laid["block_mask"] = ((2 * pair_half + batches)[:, None] == np.arange(4)).astype(np.float32)
    laid["half_ones"] = (halves[:, None] == pair_half[:32]).astype(np.float32)
    laid["mask_i_keys"] = by_query(a["mask_BxS2_ik0"])
    for n, (wq, wk, wv, wo) in {
        1: (a["L1_xattn_q_w"].T, a["L1_xattn_k_w"].T, a["L1_xattn_v_w"].T, np.eye(P, dtype=np.float32)),
        2: (a["L2_xattn_Wq"], a["L2_xattn_Wk"], a["L2_xattn_Wv"], a["L2_xattn_Wo"]),
        3: (a["L3_xattn_q_w"].T, a["L3_xattn_k_w"].T, a["L3_xattn_v_w"].T, a["L3_xattn_o_w"].T),
    }.items():
        laid[f"attn{n}_wq"], laid[f"attn{n}_wk"], laid[f"attn{n}_wv"] = wq, wk, wv
        laid[f"attn{n}_wo"] = twice_rows(wo)
    column = lambda v: v.reshape(-1, P).T
    row = lambda v: np.broadcast_to(v[None, :], (P, v.shape[0]))
    laid["attn1_bq"], laid["attn1_bk"] = column(a["L1_xattn_q_b"]), column(a["L1_xattn_k_b"])
    laid["attn1_bo"] = row(a["L1_xattn_v_b"])
    laid["attn2_bq"], laid["attn2_bk"] = column(a["L2_xattn_bq"]), column(a["L2_xattn_bk"])
    laid["attn2_bv"], laid["attn2_bo"] = row(a["L2_xattn_bv"]), row(a["L2_xattn_bo"])
    laid["attn3_bq"], laid["attn3_bk"] = column(a["L3_xattn_q_b"]), column(a["L3_xattn_k_b"])
    laid["attn3_bv"] = row(a["L3_xattn_v_b"]).T
    laid["attn3_bo"] = row(a["L3_xattn_o_b"])
    laid["attn3_wo_plain"] = a["L3_xattn_o_w"].T

    laid["numbers"] = np.broadcast_to(np.arange(EXPERTS, dtype=np.float32), (P, EXPERTS))
    token = np.arange(P)
    earlier = (token[:, None] // SEQ == token[None, :] // SEQ) & (token[:, None] < token[None, :])
    laid["earlier"] = earlier.astype(np.float32)
    laid["moe0_rw1"], laid["moe0_rb1"] = a["L0_ffn_rW1"], column(a["L0_ffn_rb1"])
    laid["moe0_rw2"], laid["moe0_rb2"] = by_group(a["L0_ffn_rW2"]), column(a["L0_ffn_rb2"])
    laid["moe0_rw"], laid["moe0_rb"] = by_group(a["L0_ffn_rW3"]), a["L0_ffn_rb3"][:, None]
    laid["moe0_w1"], laid["moe0_b1"] = a["L0_ffn_eW1"].transpose(1, 0, 2), column(a["L0_ffn_eb1"])
    laid["moe0_w2"], laid["moe0_b2"] = outputs_of(a["L0_ffn_eW2"]), a["L0_ffn_eb2"]
    laid["moe2_rw"] = a["L2_ffn_router_w"].T
    laid["moe2_w1"], laid["moe2_b1"] = a["L2_ffn_w1"].transpose(2, 0, 1), column(a["L2_ffn_b1"])
    laid["moe2_w2"], laid["moe2_b2"] = outputs_of(a["L2_ffn_w2"].transpose(0, 2, 1)), a["L2_ffn_b2"]
    laid["moe3_rw"], laid["moe3_rb"] = a["L3_ffn_router_w"].T, a["L3_ffn_experts_bias"][:, None]
    with_shared = lambda shared, own: np.concatenate([a["L3_ffn_" + shared], a["L3_ffn_" + own]])
    laid["moe3_w1"] = with_shared("sw1", "w1").transpose(1, 0, 2)
    laid["moe3_w3"] = with_shared("sw3", "w3").transpose(1, 0, 2)
    laid["moe3_w2"] = outputs_of(with_shared("sw2", "w2"))
    laid["fp8_kernel"] = a["L1_ffn_kernel"]
    laid["fp8_scales"] = row(np.concatenate([a["L1_ffn_input_scale"], a["L1_ffn_kernel_scale"]]))
    laid["fp8_bias"] = row(a["L1_ffn_bias"])


    nc = bacc.Bacc("TRN2", target_bir_lowering=False, num_devices=1)
    arrays, args = {}, {}
    for name, value in laid.items():
        value = np.ascontiguousarray(value)
        arrays["in_" + name] = value
        args[name] = nc.dram_tensor("in_" + name, value.shape, mybir.dt.from_np(value.dtype), kind="ExternalInput").ap()
    out = nc.dram_tensor("out", (TOKENS, D), F32, kind="ExternalOutput").ap()
    program(nc, args, out)
    result = run_bass_kernel_spmd(nc, [arrays], core_ids=[0])
    return result.results[0]["out"].reshape(64, SEQ, D)
```

```python
from contextlib import ExitStack

import numpy as np

import concourse.bass as bass
from concourse import mybir

F32 = mybir.dt.float32
BF16 = mybir.dt.bfloat16
U32 = mybir.dt.uint32
I32 = mybir.dt.int32
ALU = mybir.AluOpType
ACT = mybir.ActivationFunctionType
AX = mybir.AxisListType.X

P = 128
SEQ = 64
D = 128
TOKENS = 64 * SEQ
TILES = TOKENS // P
HEADS = 16
PAIRS = HEADS // 2
UNIT = 4
UNITS = TILES // UNIT
UTOK = UNIT * P
EXPERTS = 8
BANKS = 8
RING = 4
DMA_INC = 16
EPS = 1e-5
CAPACITY = int(SEQ / EXPERTS * 1.25)
MASKED = -1e30


GROUPS = {
    "ctx": [("ident", [P, P], F32), ("ctx_t", [P, TILES, P], F32)],
    "wide": [("mask_f_col", [P, TILES], F32), ("mask_f_keys", [P, TILES, SEQ], F32),
             ("wide_wq", [P, 1024], F32), ("wide_wk", [P, 1024], F32), ("wide_wv", [P, 1024], F32),
             ("wide_wo", [P, 8, P], F32)],
    "const": [("head_mask", [P, HEADS], F32), ("batch_mask", [P, 2], F32), ("block_mask", [P, 4], F32),
              ("half_ones", [P, 32], F32)],
    "mask_i": [("mask_i_rows", [2, TILES, SEQ], I32), ("batch_rows", [2, P], F32)],
    "attn1": [("attn1_wq", [P, P], F32), ("attn1_wk", [P, P], F32), ("attn1_wv", [P, P], F32),
              ("attn1_wo", [P, 2, P], F32), ("attn1_bq", [P, 1], F32), ("attn1_bk", [P, 1], F32),
              ("attn1_bo", [P, P], F32)],
    "attn2": [("attn2_wq", [P, P], F32), ("attn2_wk", [P, P], F32), ("attn2_wv", [P, P], F32),
              ("attn2_wo", [P, 2, P], F32), ("attn2_bq", [P, 1], F32), ("attn2_bk", [P, 1], F32),
              ("attn2_bv", [P, P], F32), ("attn2_bo", [P, P], F32)],
    "attn3": [("attn3_wq", [P, P], F32), ("attn3_wk", [P, P], F32), ("attn3_wv", [P, P], F32),
              ("attn3_wo", [P, 2, P], F32), ("attn3_wo_plain", [P, P], F32), ("attn3_bq", [P, 1], F32),
              ("attn3_bk", [P, 1], F32), ("attn3_bv", [P, P], F32), ("attn3_bo", [P, P], F32)],
    "moe_const": [("numbers", [P, EXPERTS], F32), ("earlier", [P, P], F32), ("slot_key", [P, 2 * CAPACITY], F32)],
    "moe0": [("moe0_rw1", [P, 512], F32), ("moe0_rb1", [P, 4], F32), ("moe0_rw2", [P, 4, 512], F32),
             ("moe0_rb2", [P, 4], F32), ("moe0_rw", [P, 4, EXPERTS], F32), ("moe0_rb", [EXPERTS, 1], F32),
             ("moe0_w1", [P, EXPERTS, 512], F32), ("moe0_b1", [P, 4 * EXPERTS], F32),
             ("moe0_w2", [P, EXPERTS, 4, P], F32), ("moe0_b2", [P, EXPERTS], F32)],
    "moe2": [("moe2_rw", [P, EXPERTS], F32), ("moe2_w1", [P, EXPERTS, 512], F32), ("moe2_b1", [P, 4 * EXPERTS], F32),
             ("moe2_w2", [P, EXPERTS, 4, P], F32), ("moe2_b2", [EXPERTS, P], F32)],
    "moe3": [("moe3_rw", [P, EXPERTS], F32), ("moe3_rb", [EXPERTS, 1], F32), ("moe3_w1", [P, EXPERTS + 1, 256], F32),
             ("moe3_w3", [P, EXPERTS + 1, 256], F32), ("moe3_w2", [P, EXPERTS + 1, 2, P], F32)],
    "fp8": [("fp8_kernel", [P, P], BF16), ("fp8_scales", [P, 2], F32), ("fp8_bias", [P, P], BF16)],
}


class Step:

    def __init__(self, i, off, stride=2):
        self.i, self.off, self.stride = i, off, stride

    def minus(self, n):
        return Step(self.i, self.off - n, self.stride)

    def at(self, k, c):
        rest = k * self.off + c
        if self.i is None:
            return rest
        by = self.i * (self.stride * k)
        return by + rest if rest >= 0 else by - (-rest)

    def inside(self, n):
        return self.i is not None or 0 <= self.off < n

    def past(self, n):
        return self.i is not None or self.off >= n

    @property
    def parity(self):
        return self.off % 2


def pipelined(eng, n, lag, body):
    first = lag + lag % 2
    for s in range(first):
        body(Step(None, s))
    with eng.Fori(first // 2, n // 2) as i:
        for off in range(2):
            body(Step(i, off))
    for s in range(n, n + lag):
        body(Step(None, s))


def tile_of(buffer, u, k=1, c=0):
    at = u.at(k, c)
    if isinstance(at, int):
        return buffer[:, at, :]
    return buffer[:, bass.ds(at, 1), :].rearrange("p a c -> p (a c)")


class Core:

    def __init__(self, nc, stack, args):
        self.nc, self.stack, self.args = nc, stack, args
        self.bank = [stack.enter_context(nc.psum_tensor(f"bank{n}", [P, 512], F32)) for n in range(BANKS)]
        self.x = self.sb("x", [P, TILES, D])
        self.stats = self.sb("stats", [P, TILES, 6])
        self.mean = self.sb("mean", [P, TILES])
        self.rstd = self.sb("rstd", [P, TILES])
        self.apart, self.std, self.half, self.var = (self.sb("norm_" + n, [P, TILES]) for n in ("apart", "std", "half", "var"))
        self.var_ready, self.std_ready, self.newton = (self.sem("norm_" + n) for n in ("var_ready", "std_ready", "newton"))
        self.stage_sems = []
        self.w, self.groups, self.loaded, self.loads = {}, {}, {}, {}

    def sb(self, name, shape, dt=F32, stack=None):
        return (stack or self.stack).enter_context(self.nc.sbuf_tensor(name, shape, dt))

    def sem(self, name):
        return self.stack.enter_context(self.nc.semaphore(name))

    def stage_sem(self, name):
        self.stage_sems.append(self.nc.alloc_semaphore(name=name))
        return self.stage_sems[-1]

    def end_of_stage(self):
        self.nc.clear_and_free_semaphores(self.stage_sems)
        self.nc.all_engine_barrier()
        self.stage_sems = []


def token_stats(core, dve, ready, u):
    dve.wait_ge(ready, u.at(1, 1))
    dve.wait_ge(ready, 1)
    core.nc.vector.bn_stats(tile_of(core.stats, u), tile_of(core.x, u))


def add_and_norm(core, dve, added, u, y, base):
    x_u = tile_of(core.x, u)
    core.nc.vector.tensor_tensor(x_u, y, base if base is not None else x_u, ALU.add).then_inc(added, 1)
    token_stats(core, dve, added, u)


def norm_scale(core, nth):
    nc = core.nc
    even, odd = core.stats[:, :, 1], core.stats[:, :, 4]
    even_sq, odd_sq = core.stats[:, :, 2], core.stats[:, :, 5]
    apart, std, half, var = core.apart, core.std, core.half, core.var
    var_ready, std_ready, newton = core.var_ready, core.std_ready, core.newton
    with nc.Block() as block:

        @block.vector
        def _(dve):
            nc.vector.tensor_tensor(core.mean[:], even, odd, ALU.add)
            nc.vector.tensor_tensor(apart[:], even, odd, ALU.subtract)
            nc.vector.tensor_tensor(var[:], even_sq, odd_sq, ALU.add).then_inc(var_ready, 1)
            dve.wait_ge(var_ready, 4 * nth + 1)
            nc.vector.tensor_scalar(core.mean[:], core.mean[:], 0.5, None, ALU.mult)
            nc.vector.tensor_scalar(apart[:], apart[:], 0.5, None, ALU.mult)
            nc.vector.tensor_scalar(var[:], var[:], 1.0 / D, EPS, ALU.mult, ALU.add).then_inc(var_ready, 1)
            dve.wait_ge(var_ready, 4 * nth + 2)
            nc.vector.tensor_tensor(apart[:], apart[:], apart[:], ALU.mult).then_inc(var_ready, 1)
            dve.wait_ge(var_ready, 4 * nth + 3)
            nc.vector.tensor_tensor(var[:], var[:], apart[:], ALU.add).then_inc(var_ready, 1)
            dve.wait_ge(std_ready, nth + 1)
            nc.vector.reciprocal(core.rstd[:], std[:]).then_inc(newton, 1)
            dve.wait_ge(newton, 4 * nth + 1)
            nc.vector.tensor_tensor(half[:], core.rstd[:], core.rstd[:], ALU.mult).then_inc(newton, 1)
            dve.wait_ge(newton, 4 * nth + 2)
            nc.vector.tensor_tensor(half[:], half[:], var[:], ALU.mult).then_inc(newton, 1)
            dve.wait_ge(newton, 4 * nth + 3)
            nc.vector.tensor_scalar(half[:], half[:], -0.5, 1.5, ALU.mult, ALU.add).then_inc(newton, 1)
            dve.wait_ge(newton, 4 * nth + 4)
            nc.vector.tensor_tensor(core.rstd[:], core.rstd[:], half[:], ALU.mult)

        @block.scalar
        def _(act):
            act.wait_ge(var_ready, 4 * nth + 4)
            nc.scalar.activation(std[:], var[:], ACT.Sqrt).then_inc(std_ready, 1)


def normalize(core, u, out, rstd, sem, k=1, c=0):
    at = u.at(k, c)
    one = slice(at, at + 1) if isinstance(at, int) else bass.ds(at, 1)
    ins = core.nc.vector.tensor_scalar(out, tile_of(core.x, u, k, c), core.mean[:, one], rstd[:, one],
                                       ALU.subtract, ALU.mult)
    if sem is not None:
        ins.then_inc(sem, 1)


def allocate(core, names, stack=None):
    for group in names:
        core.groups[group] = GROUPS[group]
        core.loaded[group] = core.sem("loaded_" + group)
        core.loads[group] = DMA_INC * len(GROUPS[group])
        for name, shape, dt in GROUPS[group]:
            core.w[name] = core.sb(name + "_sb", shape, dt, stack)


def start_loads(core, queue, names):
    for group in names:
        for name, _, _ in GROUPS[group]:
            queue.dma_start(core.w[name][:], core.args[name]).then_inc(core.loaded[group], DMA_INC)


def arrived(core, eng, *names):
    for group in names:
        eng.wait_ge(core.loaded[group], core.loads[group])


def load_and_first_stats(core, names):
    nc, args = core.nc, core.args
    loaded_x = core.sem("loaded_x")
    with nc.Block() as block:

        @block.sync
        def _(sp):
            sp.dma_start(core.x[:], args["x"].rearrange("(t p) c -> p t c", p=P)).then_inc(loaded_x, DMA_INC)
            start_loads(core, sp, names)

        @block.vector
        def _(dve):
            dve.wait_ge(loaded_x, DMA_INC)

            def body(u):
                nc.vector.bn_stats(tile_of(core.stats, u), tile_of(core.x, u))

            pipelined(dve, TILES, 0, body)


def wide_attention(core):
    nc, args, w = core.nc, core.args, core.w
    hd = 64
    scale = hd ** -0.5
    groups = HEADS * hd // P
    with ExitStack() as stack:
        sb = lambda name, shape: core.sb("wide_" + name, shape, stack=stack)
        sem = lambda name: core.stage_sem("wide_" + name)
        xhat = [sb(f"xhat{n}", [P, P]) for n in range(2)]
        x_t = sb("x_t", [P, P])
        mask_row = [sb(f"mask_row{n}", [P, P]) for n in range(2)]
        ctx_m = [sb(f"ctx_m{n}", [P, P]) for n in range(2)]
        q_t = sb("q_t", [P, groups, P])
        k_bd = sb("k_bd", [P, 2, PAIRS, 2, SEQ])
        v_bd = [sb(f"v_bd{n}", [P, 2, PAIRS, 2, hd]) for n in range(2)]
        probs = sb("probs", [P, HEADS, SEQ])
        top = sb("top", [P, HEADS])
        total = sb("total", [P, HEADS])
        total_safe = sb("total_safe", [P, HEADS])
        inverse = [sb(f"inverse{n}", [P, HEADS]) for n in range(2)]
        probs_t = sb("probs_t", [P, PAIRS, P])
        heads_out = sb("heads_out", [P, HEADS, hd])
        heads_t = sb("heads_t", [P, groups, P])
        query_scale = sb("query_scale", [P, TILES])
        query_ready = sem("query_ready")

        mask_landed = [sem(f"mask_landed{n}") for n in range(2)]
        mask_used = sem("ctx_masked")
        zeroed_k, zeroed_v = sem("zeroed_k"), sem("zeroed_v")
        xhat_ready = sem("xhat_ready")
        xt_made, xt_taken = sem("xt_made"), sem("xt_taken")
        projected = sem("projected")
        qk_taken, v_taken = sem("qk_taken"), sem("v_taken")
        scored, top_ready, shifted = sem("scored"), sem("top_ready"), sem("shifted")
        exped, masked = sem("exped"), sem("masked")
        summed, safe, inverted = sem("summed"), sem("safe"), sem("inverted")
        pt_made, pt_taken = sem("pt_made"), sem("pt_taken")
        headed, normed = sem("headed"), sem("normed")
        ht_made, ht_taken = sem("ht_made"), sem("ht_taken")
        made_y = sem("made_y")
        added = sem("added")

        t_bank = core.bank[0:2]
        p_bank = core.bank[2:4]
        o_bank = core.bank[4:6]
        s_bank = core.bank[6:8]

        with nc.Block() as block:

            @block.sync
            def _(sp):
                def body(s):
                    if s.inside(TILES):
                        if s.past(2):
                            sp.wait_ge(mask_used, s.at(1, -1))
                        at = s.at(1, 0)
                        row = args["mask_f_rows"][at:at + 1, :] if isinstance(at, int) else \
                            args["mask_f_rows"][bass.ds(at, 1), :]
                        sp.dma_start(mask_row[s.parity][:], row.to_broadcast([P, P])).then_inc(mask_landed[s.parity], DMA_INC)
                pipelined(sp, TILES, 2, body)

            @block.gpsimd
            def _(pool):
                nc.gpsimd.memset(v_bd[0][:], 0.0)
                nc.gpsimd.memset(v_bd[1][:], 0.0).then_inc(zeroed_v, 1)
                arrived(core, pool, "ctx", "wide")

                def body(s):
                    if s.inside(TILES):
                        pool.wait_ge(mask_landed[s.parity], s.minus(s.parity).at(DMA_INC // 2, DMA_INC))
                        if s.past(2):
                            pool.wait_ge(projected, s.at(6, -6))
                        nc.gpsimd.tensor_tensor(ctx_m[s.parity][:], tile_of(w["ctx_t"], s), mask_row[s.parity][:],
                                                ALU.mult).then_inc(mask_used, 1)
                    u = s.minus(1)
                    if u.inside(TILES):
                        pool.wait_ge(exped, u.at(1, 1))
                        keys = tile_of(w["mask_f_keys"], u).unsqueeze(1).to_broadcast([P, HEADS, SEQ])
                        nc.gpsimd.tensor_tensor(probs[:], probs[:], keys, ALU.mult).then_inc(masked, 1)
                pipelined(pool, TILES, 2, body)

            @block.vector
            def _(dve):
                nc.vector.memset(k_bd[:], 0.0).then_inc(zeroed_k, 1)
                arrived(core, dve, "wide")
                nc.vector.tensor_tensor(query_scale[:], core.rstd[:], w["mask_f_col"][:], ALU.mult
                                        ).then_inc(query_ready, 1)
                dve.wait_ge(query_ready, 1)
                dve.wait_ge(zeroed_v, 1)

                def body(s):
                    if s.inside(TILES):
                        if s.past(2):
                            dve.wait_ge(xt_made, s.at(1, -1))
                        normalize(core, s, xhat[s.parity][:], query_scale, xhat_ready)
                    u = s.minus(1)
                    if u.inside(TILES):
                        dve.wait_ge(scored, u.at(2, 1))
                        for half in range(2):
                            if half == 1:
                                dve.wait_ge(scored, u.at(2, 2))
                            nc.vector.tensor_reduce(
                                top[:, 8 * half:8 * half + 8],
                                s_bank[half][:].rearrange("p (h k) -> p h k", k=SEQ), AX, ALU.max
                            ).then_inc(top_ready, 1)
                        dve.wait_ge(top_ready, u.at(2, 2))
                        for half in range(2):
                            h = slice(8 * half, 8 * half + 8)
                            nc.vector.tensor_tensor(
                                probs[:, h, :], s_bank[half][:].rearrange("p (h k) -> p h k", k=SEQ),
                                top[:, h].unsqueeze(2).to_broadcast([P, 8, SEQ]), ALU.subtract
                            ).then_inc(shifted, 1)
                    u = s.minus(2)
                    if u.inside(TILES):
                        dve.wait_ge(inverted, u.at(1, 1))
                        for half in range(2):
                            h = slice(8 * half, 8 * half + 8)
                            dve.wait_ge(headed, u.at(2, 1 + half))
                            nc.vector.tensor_tensor(
                                heads_out[:, h, :], o_bank[half][:].rearrange("p (h d) -> p h d", d=hd),
                                inverse[u.parity][:, h].unsqueeze(2).to_broadcast([P, 8, hd]), ALU.mult
                            ).then_inc(normed, 1)
                    if s.inside(TILES):
                        for n in range(2):
                            dve.wait_ge(projected, s.at(6, 5 + n))
                            v = p_bank[n][:].rearrange("p (hp h d) -> p hp h d", h=2, d=hd)
                            for b in range(2):
                                for h2 in range(2):
                                    ins = nc.vector.tensor_copy(
                                        v_bd[s.parity][SEQ * h2:SEQ * h2 + SEQ, b, 4 * n:4 * n + 4, h2, :],
                                        v[SEQ * b:SEQ * b + SEQ, :, h2, :])
                            ins.then_inc(v_taken, 1)
                    u = s.minus(1)
                    if u.inside(TILES):
                        dve.wait_ge(masked, u.at(1, 1))
                        nc.vector.tensor_reduce(total[:], probs[:], AX, ALU.add).then_inc(summed, 1)
                        dve.wait_ge(summed, u.at(1, 1))
                        nc.vector.scalar_tensor_tensor(total_safe[:], total[:], 0.0, total[:], ALU.is_equal, ALU.add
                                                       ).then_inc(safe, 1)
                        dve.wait_ge(safe, u.at(1, 1))
                        nc.vector.reciprocal(inverse[u.parity][:], total_safe[:]).then_inc(inverted, 1)
                    u = s.minus(2)
                    if u.inside(TILES):
                        dve.wait_ge(made_y, u.at(1, 1))
                        add_and_norm(core, dve, added, u, o_bank[0][:, 0:P], None)
                pipelined(dve, TILES, 2, body)

            @block.scalar
            def _(act):
                act.wait_ge(zeroed_k, 1)

                def body(s):
                    if s.inside(TILES):
                        act.wait_ge(xt_made, s.at(1, 1))
                        nc.scalar.copy(x_t[:], t_bank[0][:, 0:P]).then_inc(xt_taken, 1)
                        for n in range(2):
                            act.wait_ge(projected, s.at(6, 1 + n))
                            nc.scalar.copy(q_t[:, 4 * n:4 * n + 4, :].rearrange("p g t -> p (g t)"), p_bank[n][:]
                                           ).then_inc(qk_taken, 1)
                    u = s.minus(1)
                    if u.inside(TILES):
                        act.wait_ge(shifted, u.at(2, 2))
                        nc.scalar.activation(probs[:], probs[:], ACT.Exp, scale=scale).then_inc(exped, 1)
                    if s.inside(TILES):
                        for n in range(2):
                            act.wait_ge(projected, s.at(6, 3 + n))
                            k = p_bank[n][:].rearrange("p (hp b k) -> p b hp k", b=2, k=SEQ)
                            for h2 in range(2):
                                rows = slice(SEQ * h2, SEQ * h2 + SEQ)
                                ins = nc.scalar.copy(k_bd[rows, :, 4 * n:4 * n + 4, h2, :], k[rows])
                            ins.then_inc(qk_taken, 1)
                    u = s.minus(2)
                    if u.inside(TILES):
                        for n in range(2):
                            act.wait_ge(ht_made, u.at(2, 1 + n))
                            nc.scalar.copy(heads_t[:, 4 * n:4 * n + 4, :].rearrange("p g t -> p (g t)"),
                                           t_bank[1 - n][:]).then_inc(ht_taken, 1)
                    u = s.minus(1)
                    if u.inside(TILES):
                        for n in range(2):
                            act.wait_ge(pt_made, u.at(2, 1 + n))
                            nc.scalar.copy(probs_t[:, 4 * n:4 * n + 4, :].rearrange("p g t -> p (g t)"),
                                           t_bank[1 - n][:]).then_inc(pt_taken, 1)
                pipelined(act, TILES, 2, body)

            @block.tensor
            def _(pe):
                arrived(core, pe, "ctx", "wide")

                def body(s):
                    two = s.minus(2)
                    one = s.minus(1)
                    if s.inside(TILES):
                        pe.wait_ge(xhat_ready, s.at(1, 1))
                        if s.past(2):
                            pe.wait_ge(pt_taken, s.at(2, -2))
                        nc.tensor.transpose(t_bank[0][:, 0:P], xhat[s.parity][:], w["ident"][:]).then_inc(xt_made, 1)
                        pe.wait_ge(xt_taken, s.at(1, 1))
                        for n in range(2):
                            if s.past(1):
                                pe.wait_ge(v_taken, s.at(2, -1 + n))
                            for g in range(4):
                                ins = nc.tensor.matmul(p_bank[n][:, g * P:g * P + P],
                                                       w["wide_wq"][:, (4 * n + g) * P:(4 * n + g + 1) * P],
                                                       x_t[:], start=True, stop=True)
                            ins.then_inc(projected, 1)
                        pe.wait_ge(mask_used, s.at(1, 1))
                        for n in range(2):
                            pe.wait_ge(qk_taken, s.at(4, 1 + n))
                            for g in range(4):
                                ins = nc.tensor.matmul(p_bank[n][:, g * P:g * P + P],
                                                       w["wide_wk"][:, (4 * n + g) * P:(4 * n + g + 1) * P],
                                                       ctx_m[s.parity][:], start=True, stop=True)
                            ins.then_inc(projected, 1)
                        for n in range(2):
                            pe.wait_ge(qk_taken, s.at(4, 3 + n))
                            nc.tensor.matmul(p_bank[n][:], ctx_m[s.parity][:], w["wide_wv"][:, n * 512:n * 512 + 512],
                                             start=True, stop=True).then_inc(projected, 1)
                    if two.inside(TILES):
                        for n in range(2):
                            pe.wait_ge(normed, two.at(2, 1 + n))
                            if n == 0:
                                pe.wait_ge(pt_taken, two.at(2, 1))
                            elif s.inside(TILES):
                                pe.wait_ge(xt_taken, s.at(1, 1))
                            else:
                                pe.wait_ge(pt_taken, two.at(2, 2))
                            for g in range(4):
                                f = 4 * n + g
                                ins = nc.tensor.transpose(t_bank[1 - n][:, g * P:g * P + P],
                                                          heads_out[:, 2 * f:2 * f + 2, :].rearrange("p h d -> p (h d)"),
                                                          w["ident"][:])
                            ins.then_inc(ht_made, 1)
                    if one.inside(TILES):
                        pe.wait_ge(masked, one.at(1, 1))
                        for n in range(2):
                            if two.inside(TILES):
                                pe.wait_ge(ht_taken, two.at(2, 1 + n))
                            elif n == 1 and s.inside(TILES):
                                pe.wait_ge(xt_taken, s.at(1, 1))
                            for g in range(4):
                                f = 4 * n + g
                                ins = nc.tensor.transpose(t_bank[1 - n][:, g * P:g * P + P],
                                                          probs[:, 2 * f:2 * f + 2, :].rearrange("p h k -> p (h k)"),
                                                          w["ident"][:])
                            ins.then_inc(pt_made, 1)
                    if two.inside(TILES):
                        pe.wait_ge(ht_taken, two.at(2, 2))
                        for g in range(groups):
                            ins = nc.tensor.matmul(o_bank[0][:, 0:P], heads_t[:, g, :], w["wide_wo"][:, g, :],
                                                   start=(g == 0), stop=(g == groups - 1))
                        ins.then_inc(made_y, 1)
                    if s.inside(TILES):
                        pe.wait_ge(qk_taken, s.at(4, 4))
                        if s.past(1):
                            pe.wait_ge(shifted, s.at(2, 0))
                        for n in range(2):
                            for g in range(4):
                                for b in range(2):
                                    ins = nc.tensor.matmul(
                                        s_bank[n][SEQ * b:SEQ * b + SEQ, g * P:g * P + P],
                                        q_t[:, 4 * n + g, SEQ * b:SEQ * b + SEQ],
                                        k_bd[:, b, 4 * n + g].rearrange("p h k -> p (h k)"), start=True, stop=True)
                            ins.then_inc(scored, 1)
                    if one.inside(TILES):
                        pe.wait_ge(pt_taken, one.at(2, 2))
                        pe.wait_ge(v_taken, one.at(2, 2))
                        if two.inside(TILES):
                            pe.wait_ge(added, two.at(1, 1))
                        for n in range(2):
                            for g in range(4):
                                for b in range(2):
                                    ins = nc.tensor.matmul(
                                        o_bank[n][SEQ * b:SEQ * b + SEQ, g * P:g * P + P],
                                        probs_t[:, 4 * n + g, SEQ * b:SEQ * b + SEQ],
                                        v_bd[one.parity][:, b, 4 * n + g].rearrange("p h d -> p (h d)"),
                                        start=True, stop=True)
                            ins.then_inc(headed, 1)
                pipelined(pe, TILES, 2, body)


def narrow_attention(core, name, over_keys, masked_keys, keys_first=False):
    nc, w = core.nc, core.w
    hd = D // HEADS
    scale = hd ** -0.5
    with ExitStack() as stack:
        sb = lambda n, shape: core.sb(f"{name}_{n}", shape, stack=stack)
        sem = lambda n: core.stage_sem(f"{name}_{n}")
        xhat = [sb(f"xhat{n}", [P, P]) for n in range(2)]
        x_t = sb("x_t", [P, P])
        context = [sb(f"context{n}", [P, 2, 2 if over_keys else 1, SEQ]) for n in range(2)]
        row_t = [sb(f"row_t{n}", [P, P]) for n in range(2)]
        col_t = [sb(f"col_t{n}", [P, P]) for n in range(2)]
        col_bd = sb("col_bd", [P, 2, HEADS, SEQ])
        probs = [sb(f"probs{n}", [P, HEADS, SEQ]) for n in range(2)]
        top = sb("top", [P, HEADS])
        v_bd = [sb(f"v_bd{n}", [P, PAIRS, 2, 2, hd]) for n in range(2)]
        heads_t = sb("heads_t", [P, 2, P])
        rows_w = sb("rows_w", [P, 2, 2, P] if over_keys else [P, 2, 2, 2, P])
        based = [sb(f"based{n}", [P, P]) for n in range(2)]
        constant = sb("constant", [P, P])
        if over_keys:
            probs_t = sb("probs_t", [P, PAIRS, P])
            inverse_t = sb("inverse_t", [P, 2, P])
        else:
            total = sb("total", [P, HEADS])
            inverse = sb("inverse", [P, HEADS])
            v_biased = [sb(f"v_biased{n}", [P, P]) for n in range(2)]

        zeroed, weighted, const_made, const_ready = sem("zeroed"), sem("weighted"), sem("const_made"), sem("const_ready")
        staged, base_ready = sem("staged"), sem("base_ready")
        xhat_ready, xt_made, xt_taken = sem("xhat_ready"), sem("xt_made"), sem("xt_taken")
        projected, qk_taken = sem("projected"), sem("qk_taken")
        spread_a, spread_b = sem("spread_a"), sem("spread_b")
        v_made, v_taken = sem("v_made"), sem("v_taken")
        scored, masked, top_ready, shifted, exped = sem("scored"), sem("masked"), sem("top_ready"), sem("shifted"), sem("exped")
        pt_made, pt_taken = sem("pt_made"), sem("pt_taken")
        headed, ht_ready = sem("headed"), sem("ht_ready")
        inverted, summed, scaled = sem("inverted"), sem("summed"), sem("scaled")
        made_y, y_free, added = sem("made_y"), sem("y_free"), sem("added")

        q_bank = core.bank[0]
        v_bank = core.bank[1]
        s_bank = core.bank[2:4]
        pt_bank = core.bank[4:6]
        h_bank = core.bank[6]
        y_bank = core.bank[7]
        row_w, col_w = (name + "_wq", name + "_wk") if over_keys else (name + "_wk", name + "_wq")
        row_b, col_b = (name + "_bq", name + "_bk") if over_keys else (name + "_bk", name + "_bq")
        def spread(s, b):
            shape = [P, HEADS, SEQ]
            return (col_bd[:, b], col_t[s.parity][:, SEQ * b:SEQ * b + SEQ].unsqueeze(1).to_broadcast(shape),
                    w["head_mask"][:].unsqueeze(2).to_broadcast(shape))

        with nc.Block() as block:

            @block.gpsimd
            def _(pool):
                nc.gpsimd.memset(v_bd[0][:], 0.0)
                nc.gpsimd.memset(v_bd[1][:], 0.0).then_inc(zeroed, 1)
                arrived(core, pool, "ctx", "const")
                pool.wait_ge(const_ready, 1)

                def body(s):
                    u = s.minus(2)
                    if u.inside(TILES):
                        if not over_keys:
                            pool.wait_ge(inverted, u.at(1, 1))
                            for b in range(2):
                                rows = slice(SEQ * b, SEQ * b + SEQ)
                                if b == 1:
                                    pool.wait_ge(scaled, u.at(2, 1))
                                elif u.past(2):
                                    pool.wait_ge(base_ready, u.at(1, -1))
                                else:
                                    pool.wait_ge(spread_b, u.at(1, 2))
                                nc.gpsimd.tensor_tensor(
                                    v_bd[u.parity][rows, :, b],
                                    v_biased[u.parity][rows].rearrange("p (hp h d) -> p hp h d", h=2, d=hd),
                                    inverse[rows].rearrange("p (hp h) -> p hp h", h=2).unsqueeze(3)
                                    .to_broadcast([SEQ, PAIRS, 2, hd]), ALU.mult).then_inc(scaled, 1)
                            pool.wait_ge(scaled, u.at(2, 2))
                    if s.inside(TILES):
                        pool.wait_ge(qk_taken, s.at(2, 2))
                        if s.past(1):
                            pool.wait_ge(scored, s.at(2, 0))
                        nc.gpsimd.tensor_tensor(*spread(s, 1), ALU.mult).then_inc(spread_b, 1)
                    u = s.minus(3)
                    if u.inside(TILES):
                        if u.past(2):
                            pool.wait_ge(added, u.at(1, -1))
                        nc.gpsimd.tensor_tensor(based[u.parity][:], tile_of(core.x, u), constant[:], ALU.add
                                                ).then_inc(base_ready, 1)
                pipelined(pool, TILES, 3, body)

            @block.vector
            def _(dve):
                arrived(core, dve, "const", name)
                dve.sem_inc(y_free, 1)
                for g in range(2):
                    for b in range(2):
                        for x in range(1 if over_keys else 2):
                            out = rows_w[:, g, b] if over_keys else rows_w[:, g, x, b]
                            mask = w["batch_mask"][:, b:b + 1] if over_keys else w["block_mask"][:, 2 * x + b:2 * x + b + 1]
                            ins = nc.vector.tensor_scalar(out, w[name + "_wo"][:, g], mask, None, ALU.mult)
                ins.then_inc(weighted, 1)
                if name == "attn3":
                    dve.wait_ge(const_made, 1)
                    nc.vector.tensor_tensor(constant[:], y_bank[:, 0:P], w["attn3_bo"][:], ALU.add).then_inc(const_ready, 1)
                else:
                    nc.vector.tensor_copy(constant[:], w[name + "_bo"][:]).then_inc(const_ready, 1)
                dve.wait_ge(zeroed, 1)

                def body(s):
                    if s.inside(TILES):
                        if s.past(2):
                            dve.wait_ge(xt_made, s.at(1, -1))
                        normalize(core, s, xhat[s.parity][:], core.rstd, xhat_ready)
                    u = s.minus(3)
                    if u.inside(TILES) and over_keys:
                        dve.wait_ge(headed, u.at(1, 1))
                        flat = "p g t -> p (g t)"
                        nc.vector.reciprocal(inverse_t[:].rearrange(flat), h_bank[:, 256:512]).then_inc(inverted, 1)
                        dve.wait_ge(inverted, u.at(1, 1))
                        nc.vector.tensor_tensor(heads_t[:].rearrange(flat), h_bank[:, 0:256],
                                                inverse_t[:].rearrange(flat), ALU.mult).then_inc(ht_ready, 1)
                    u = s.minus(2)
                    if u.inside(TILES) and not over_keys:
                        dve.wait_ge(exped, u.at(1, 1))
                        nc.vector.tensor_reduce(total[:], probs[u.parity][:], AX, ALU.add).then_inc(summed, 1)
                        dve.wait_ge(summed, u.at(1, 1))
                        if u.past(1):
                            dve.wait_ge(scaled, u.at(2, 0))
                        nc.vector.reciprocal(inverse[:], total[:]).then_inc(inverted, 1)
                    u = s.minus(1)
                    if u.inside(TILES):
                        for half in range(2):
                            dve.wait_ge(scored, u.at(2, 1 + half))
                            nc.vector.tensor_reduce(top[:, 8 * half:8 * half + 8],
                                                    s_bank[half][:].rearrange("p (h k) -> p h k", k=SEQ), AX, ALU.max
                                                    ).then_inc(top_ready, 1)
                        dve.wait_ge(top_ready, u.at(2, 2))
                        for half in range(2):
                            h = slice(8 * half, 8 * half + 8)
                            ins = nc.vector.tensor_tensor(
                                probs[u.parity][:, h], s_bank[half][:].rearrange("p (h k) -> p h k", k=SEQ),
                                top[:, h].unsqueeze(2).to_broadcast([P, 8, SEQ]), ALU.subtract)
                        ins.then_inc(shifted, 1)
                        if not over_keys:
                            dve.wait_ge(v_made, u.at(1, 1))
                            if u.past(2):
                                dve.wait_ge(scaled, u.at(2, -2))
                            nc.vector.tensor_tensor(v_biased[u.parity][:], v_bank[:, 0:P], w[name + "_bv"][:], ALU.add
                                                    ).then_inc(v_taken, 1)
                    if s.inside(TILES):
                        dve.wait_ge(qk_taken, s.at(2, 2))
                        nc.vector.tensor_tensor(*spread(s, 0), ALU.mult).then_inc(spread_a, 1)
                    u = s.minus(3)
                    if u.inside(TILES):
                        dve.wait_ge(made_y, u.at(1, 1))
                        dve.wait_ge(base_ready, u.at(1, 1))
                        x_u = tile_of(core.x, u)
                        nc.vector.tensor_tensor(x_u, y_bank[:, 0:P], based[u.parity][:], ALU.add).then_inc(added, 1)
                        token_stats(core, dve, added, u)
                pipelined(dve, TILES, 3, body)

            @block.scalar
            def _(act):
                arrived(core, act, "ctx", name)
                act.wait_ge(zeroed, 1)

                def body(s):
                    if s.inside(TILES):
                        if s.past(2):
                            act.wait_ge(v_made, s.at(1, -1))
                        tile = tile_of(w["ctx_t"], s).rearrange("p (b k) -> p b k", b=2)
                        for twice in range(2 if over_keys else 1):
                            ins = nc.scalar.copy(context[s.parity][:, :, twice, :], tile)
                        ins.then_inc(staged, 1)
                    u = s.minus(3)
                    if u.inside(TILES) and not over_keys:
                        act.wait_ge(headed, u.at(1, 1))
                        nc.scalar.copy(heads_t[:].rearrange("p g t -> p (g t)"), h_bank[:, 0:256]).then_inc(ht_ready, 1)
                    if s.inside(TILES):
                        act.wait_ge(xt_made, s.at(1, 1))
                        nc.scalar.copy(x_t[:], q_bank[:, 0:P]).then_inc(xt_taken, 1)
                        act.wait_ge(projected, s.at(1, 1))
                        if s.past(2):
                            act.wait_ge(scored, s.at(2, -2))
                        nc.scalar.activation(row_t[s.parity][:], q_bank[:, P:2 * P], ACT.Identity, bias=w[row_b][:, 0:1]
                                             ).then_inc(qk_taken, 1)
                        nc.scalar.activation(col_t[s.parity][:], q_bank[:, 2 * P:3 * P], ACT.Identity, bias=w[col_b][:, 0:1]
                                             ).then_inc(qk_taken, 1)
                    u = s.minus(2)
                    if u.inside(TILES) and over_keys:
                        for n in range(2):
                            act.wait_ge(pt_made, u.at(2, 1 + n))
                            nc.scalar.copy(probs_t[:, 4 * n:4 * n + 4, :].rearrange("p g t -> p (g t)"), pt_bank[n][:]
                                           ).then_inc(pt_taken, 1)
                    u = s.minus(1)
                    if u.inside(TILES):
                        if over_keys:
                            act.wait_ge(v_made, u.at(1, 1))
                            v = v_bank[:, 0:256].rearrange("p (b hp h d) -> p b hp h d", b=2, hp=PAIRS, h=2)
                            for h2 in range(2):
                                rows = slice(SEQ * h2, SEQ * h2 + SEQ)
                                for b in range(2):
                                    ins = nc.scalar.copy(v_bd[u.parity][rows, :, b, h2, :], v[rows, b, :, h2, :])
                            ins.then_inc(v_taken, 1)
                        act.wait_ge(shifted, u.at(1, 1))
                        nc.scalar.activation(probs[u.parity][:], probs[u.parity][:], ACT.Exp, scale=scale).then_inc(exped, 1)
                pipelined(act, TILES, 3, body)

            @block.tensor
            def _(pe):
                arrived(core, pe, "ctx", "const", name)
                if name == "attn3":
                    pe.wait_ge(weighted, 1)
                    nc.tensor.matmul(y_bank[:, 0:P], w["attn3_bv"][:], w["attn3_wo_plain"][:], start=True, stop=True
                                     ).then_inc(const_made, 1)
                pe.wait_ge(weighted, 1)
                pe.wait_ge(const_ready, 1)

                def body(s):
                    u = s.minus(1)
                    if u.inside(TILES):
                        pe.wait_ge(spread_a, u.at(1, 1))
                        pe.wait_ge(spread_b, u.at(1, 1))
                        if u.past(1):
                            pe.wait_ge(shifted, u.at(1, 0))
                        for n in range(2):
                            if masked_keys:
                                keys = tile_of(w["minus_huge"], u).unsqueeze(1).to_broadcast([2, 8, SEQ])
                                nc.tensor.matmul(s_bank[n][:], w["batch_rows_bf"][:], keys, start=True, stop=False)
                            for b in range(2):
                                ins = nc.tensor.matmul(
                                    s_bank[n][SEQ * b:SEQ * b + SEQ, :], row_t[u.parity][:, SEQ * b:SEQ * b + SEQ],
                                    col_bd[:, b, 8 * n:8 * n + 8].rearrange("p h k -> p (h k)"),
                                    start=not masked_keys, stop=True)
                            ins.then_inc(scored, 1)
                    if s.inside(TILES):
                        pe.wait_ge(xhat_ready, s.at(1, 1))
                        if s.past(1):
                            pe.wait_ge(qk_taken, s.at(2, 0))
                        nc.tensor.transpose(q_bank[:, 0:P], xhat[s.parity][:], w["ident"][:]).then_inc(xt_made, 1)
                    u = s.minus(1)
                    if u.inside(TILES):
                        if u.past(1):
                            pe.wait_ge(v_taken, u.at(1, 0))
                        if over_keys:
                            for b in range(2):
                                ins = nc.tensor.matmul(v_bank[:, b * P:b * P + P],
                                                       context[u.parity][:, b].rearrange("p t k -> p (t k)"),
                                                       w[name + "_wv"][:], start=True, stop=True)
                        else:
                            ins = nc.tensor.matmul(v_bank[:, 0:P], context[u.parity][:].rearrange("p b t k -> p (b t k)"),
                                                   w[name + "_wv"][:],
                                                   start=True, stop=True)
                        ins.then_inc(v_made, 1)
                    if s.inside(TILES):
                        pe.wait_ge(xt_taken, s.at(1, 1))
                        pe.wait_ge(staged, s.at(1, 1))
                        ctx_rhs = context[s.parity][:, :, 0]
                        rows, cols = (x_t[:], ctx_rhs) if over_keys else (ctx_rhs, x_t[:])
                        nc.tensor.matmul(q_bank[:, P:2 * P], w[row_w][:], rows, start=True, stop=True)
                        nc.tensor.matmul(q_bank[:, 2 * P:3 * P], w[col_w][:], cols, start=True, stop=True
                                         ).then_inc(projected, 1)
                    u = s.minus(2)
                    if u.inside(TILES) and over_keys:
                        pe.wait_ge(exped, u.at(1, 1))
                        for n in range(2):
                            if u.past(1):
                                pe.wait_ge(pt_taken, u.at(2, -1 + n))
                            for g in range(4):
                                f = 4 * n + g
                                ins = nc.tensor.transpose(
                                    pt_bank[n][:, g * P:g * P + P],
                                    probs[u.parity][:, 2 * f:2 * f + 2, :].rearrange("p h k -> p (h k)"), w["ident"][:])
                            ins.then_inc(pt_made, 1)
                    u = s.minus(3)
                    if u.inside(TILES):
                        pe.wait_ge(ht_ready, u.at(1, 1))
                        pe.wait_ge(y_free, 1)
                        if u.past(1):
                            pe.wait_ge(added, u.at(1, 0))
                        terms = [(g, x) for g in range(2) for x in range(1 if over_keys else 2)]
                        for n, (g, x) in enumerate(terms):
                            for b in range(2):
                                at = SEQ * (b if over_keys else x)
                                ins = nc.tensor.matmul(
                                    y_bank[SEQ * b:SEQ * b + SEQ, 0:P], heads_t[:, g, at:at + SEQ],
                                    rows_w[:, g, b] if over_keys else rows_w[:, g, x, b],
                                    start=(n == 0), stop=(n == len(terms) - 1))
                        ins.then_inc(made_y, 1)
                    u = s.minus(2)
                    if u.inside(TILES):
                        if over_keys:
                            pe.wait_ge(v_taken, u.at(1, 1))
                        else:
                            pe.wait_ge(scaled, u.at(2, 2))
                        for g in range(2):
                            if over_keys:
                                pe.wait_ge(pt_taken, u.at(2, 1 + g))
                            for j in range(4):
                                hp = 4 * g + j
                                rhs = probs_t[:, hp, :] if over_keys else \
                                    probs[u.parity][:, 2 * hp:2 * hp + 2, :].rearrange("p h l -> p (h l)")
                                ins = nc.tensor.matmul(
                                    h_bank[32 * j:32 * j + 32, g * P:g * P + P],
                                    v_bd[u.parity][:, hp].rearrange("p b h d -> p (b h d)"), rhs, start=True, stop=True)
                        if over_keys:
                            for g in range(2):
                                for j in range(4):
                                    ins = nc.tensor.matmul(h_bank[32 * j:32 * j + 32, (2 + g) * P:(3 + g) * P],
                                                           w["half_ones"][:], probs_t[:, 4 * g + j, :], start=True, stop=True)
                        ins.then_inc(headed, 1)
                pipelined(pe, TILES, 3, body)


def prepare_mask(core):
    nc, w = core.nc, core.w
    with nc.Block() as block:

        @block.vector
        def _(dve):
            arrived(core, dve, "mask_i")
            nc.vector.tensor_copy(w["batch_rows_bf"][:], w["batch_rows"][:])
            nc.vector.tensor_scalar(w["minus_huge"][:], w["mask_i_rows"][:], 0.0, MASKED, ALU.is_gt, ALU.mult)


def unit_of(buffer, u):
    at = u.at(UNIT, 0)
    span = slice(at, at + UNIT) if isinstance(at, int) else bass.ds(at, UNIT)
    return buffer[:, span, :].rearrange("p a c -> p (a c)")


def units(eng, body):
    with eng.Fori(0, UNITS) as i:
        body(Step(i, 0, 1))


def units_ahead(eng, ahead, body):
    ahead(Step(None, 0))
    with eng.Fori(0, UNITS - 1) as i:
        u = Step(i, 0, 1)
        body(u, lambda: ahead(u.minus(-1)))
    body(Step(None, UNITS - 1), lambda: None)


def quantize(core, eng, done, count, value, parts, out):
    nc = core.nc
    power, rounded = parts
    nc.vector.tensor_scalar(power.bitcast(U32), value.bitcast(U32), 0x7F800000, None, ALU.bitwise_and).then_inc(done, 1)
    eng.wait_ge(done, count(1))
    nc.vector.tensor_scalar(power, power, 2.0 ** -6, 1.5 * 2.0 ** 20, ALU.max, ALU.mult).then_inc(done, 1)
    eng.wait_ge(done, count(2))
    nc.vector.tensor_tensor(rounded, value, power, ALU.add).then_inc(done, 1)
    eng.wait_ge(done, count(3))
    nc.vector.tensor_tensor(rounded, rounded, power, ALU.subtract).then_inc(done, 1)
    eng.wait_ge(done, count(4))
    nc.vector.tensor_scalar(power, rounded, 2.0 ** 64 / 470 * 2.0 ** 64, 0.0, ALU.mult, ALU.mult).then_inc(done, 1)
    eng.wait_ge(done, count(5))
    nc.vector.tensor_tensor(out, rounded, power, ALU.add).then_inc(done, 1)


QUANTIZE_STEPS = 6


def fp8_product(core):
    nc, w = core.nc, core.w
    with ExitStack() as stack:
        sb = lambda n, shape, dt=F32: core.sb("fp8_" + n, shape, dt, stack)
        sem = lambda n: core.stage_sem("fp8_" + n)
        x_bf = sb("x_bf", [P, UNIT, P], BF16)
        value, power, rounded = (sb(n, [P, UTOK]) for n in ("value", "power", "rounded"))
        x_q = sb("x_q", [P, UTOK], BF16)
        x_qt = sb("x_qt", [P, UTOK], BF16)
        kernel_q = sb("kernel_q", [P, P], BF16)
        ident_bf = sb("ident_bf", [P, P], BF16)
        inverses = sb("inverses", [P, 2])
        product = sb("product", [P, 1])
        y_bf, y_biased = sb("y_bf", [P, UTOK], BF16), sb("y_biased", [P, UTOK], BF16)

        prepared, k_rounding, normed = sem("prepared"), sem("k_rounding"), sem("normed")
        rounding, xt_made, xt_taken = sem("rounding"), sem("xt_made"), sem("xt_taken")
        made_y, y_cast, y_summed, added = sem("made_y"), sem("y_cast"), sem("y_summed"), sem("added")
        t_bank, y_bank = core.bank[0], core.bank[1]
        t_bf = t_bank[:].bitcast(BF16)[:, 0:UTOK]

        with nc.Block() as block:

            @block.vector
            def _(dve):
                arrived(core, dve, "fp8", "ctx")
                nc.vector.tensor_copy(ident_bf[:], w["ident"][:])
                nc.vector.tensor_tensor(product[:], w["fp8_scales"][:, 0:1], w["fp8_scales"][:, 1:2], ALU.mult)
                nc.vector.reciprocal(inverses[:], w["fp8_scales"][:]).then_inc(prepared, 1)
                dve.wait_ge(prepared, 1)
                nc.vector.tensor_scalar(value[:, 0:P], w["fp8_kernel"][:], inverses[:, 1:2], None, ALU.mult).then_inc(prepared, 1)
                dve.wait_ge(prepared, 2)
                dve.sem_inc(y_cast, 1)
                quantize(core, dve, k_rounding, lambda n: n, value[:, 0:P], (power[:, 0:P], rounded[:, 0:P]), kernel_q[:])
                dve.wait_ge(k_rounding, QUANTIZE_STEPS)

                def ahead(u):
                    for t in range(UNIT):
                        normalize(core, u, x_bf[:, t], core.rstd, normed if t == UNIT - 1 else None, UNIT, t)
                    dve.wait_ge(normed, u.at(2, 1))
                    nc.vector.tensor_scalar(value[:], x_bf[:].rearrange("p t c -> p (t c)"), inverses[:, 0:1], None, ALU.mult
                                            ).then_inc(normed, 1)
                    dve.wait_ge(normed, u.at(2, 2))
                    if u.i is not None or u.off:
                        dve.wait_ge(xt_made, u.at(1, 0))
                    quantize(core, dve, rounding, lambda n: u.at(QUANTIZE_STEPS, n), value[:], (power[:], rounded[:]), x_q[:])

                def body(u, then):
                    then()
                    dve.wait_ge(made_y, u.at(1, 1))
                    nc.vector.tensor_scalar(y_bf[:], y_bank[:], product[:, 0:1], None, ALU.mult).then_inc(y_cast, 1)
                    dve.wait_ge(y_cast, u.at(1, 2))
                    nc.vector.tensor_tensor(y_biased[:].rearrange("p (t c) -> p t c", t=UNIT),
                                            y_bf[:].rearrange("p (t c) -> p t c", t=UNIT),
                                            w["fp8_bias"][:].unsqueeze(1).to_broadcast([P, UNIT, P]), ALU.add).then_inc(y_summed, 1)
                    dve.wait_ge(y_summed, u.at(1, 1))
                    nc.vector.tensor_tensor(unit_of(core.x, u), unit_of(core.x, u), y_biased[:], ALU.add).then_inc(added, 1)
                    unit_stats(core, dve, added, u)
                units_ahead(dve, ahead, body)

            @block.scalar
            def _(act):
                def body(u):
                    act.wait_ge(xt_made, u.at(1, 1))
                    nc.scalar.copy(x_qt[:], t_bf).then_inc(xt_taken, 1)
                units(act, body)

            @block.tensor
            def _(pe):
                pe.wait_ge(k_rounding, QUANTIZE_STEPS)

                def body(u):
                    pe.wait_ge(rounding, u.at(QUANTIZE_STEPS, QUANTIZE_STEPS))
                    for t in range(UNIT):
                        ins = nc.tensor.transpose(t_bf[:, t * P:t * P + P], x_q[:, t * P:t * P + P], ident_bf[:])
                    ins.then_inc(xt_made, 1)
                    pe.wait_ge(xt_taken, u.at(1, 1))
                    pe.wait_ge(y_cast, u.at(1, 1))
                    for t in range(UNIT):
                        ins = nc.tensor.matmul(y_bank[:, t * P:t * P + P], x_qt[:, t * P:t * P + P], kernel_q[:],
                                               start=True, stop=True)
                    ins.then_inc(made_y, 1)
                units(pe, body)


def unit_stats(core, dve, added, u):
    dve.wait_ge(added, u.at(1, 1))
    dve.wait_ge(added, 1)
    for t in range(UNIT):
        core.nc.vector.bn_stats(tile_of(core.stats, u, UNIT, t), tile_of(core.x, u, UNIT, t))


def experts(core, name):
    nc, w = core.nc, core.w
    gated = name == "moe3"
    biased = not gated
    n_exp = EXPERTS + gated
    nf = 2 if gated else 4
    act_fn = ACT.Silu if gated else ACT.Gelu
    uses = 0 if gated else n_exp * nf
    steps = 2 * n_exp
    flat = "p t e -> p (t e)"
    with ExitStack() as stack:
        sb = lambda n, shape, dt=F32: core.sb(f"{name}_{n}", shape, dt, stack)
        sem = lambda n: core.stage_sem(f"{name}_{n}")
        xhat = sb("xhat", [P, UNIT, P])
        x_t = sb("x_t", [P, UTOK])
        hidden = [sb(f"hidden{n}", [P, nf, UTOK]) for n in range(2)]
        if gated:
            gate = [sb(f"gate{n}", [P, UTOK]) for n in range(2)]
        logits_t = sb("logits_t", [EXPERTS, UTOK])
        score = sb("score", [P, UNIT, EXPERTS])
        best = sb("best", [P, UNIT, 8])
        index = sb("index", [P, UNIT, 8], U32)
        index_f = sb("index_f", [P, UNIT, 2])
        one_hot = sb("one_hot", [P, UNIT, 2, EXPERTS])
        chosen = sb("chosen", [P, UNIT, EXPERTS])
        weight = sb("weight", [P, UNIT, EXPERTS])
        row = sb("row", [P, UNIT])
        row_inv = sb("row_inv", [P, UNIT])
        pair_weight = sb("pair_weight", [P, UNIT, 2])
        weight_t = sb("weight_t", [EXPERTS, UTOK])

        xhat_ready, transposed, xt_taken = sem("xhat_ready"), sem("transposed"), sem("xt_taken")
        hid_made, hid_taken = sem("hid_made"), sem("hid_taken")
        gate_made, up_made, gated_ready, h_ready = sem("gate_made"), sem("up_made"), sem("gated"), sem("h_ready")
        lt_made, lt_taken, logits_made = sem("lt_made"), sem("lt_taken"), sem("logits_made")
        route, squashed = sem("route"), sem("squashed")
        settled = sem("settled")
        weighted_t, wt_taken, bias_made = sem("weights_t"), sem("wt_taken"), sem("bias_made")
        y_made, y_taken, added = sem("y_made"), sem("y_taken"), sem("added")

        t_bank, small, y_banks = core.bank[6], core.bank[7], core.bank[4:6]
        CHAIN = 11

        with nc.Block() as block:


            @block.vector
            def _(dve):
                arrived(core, dve, "ctx", name, "moe_const")
                dve.sem_inc(y_taken, 2)
                if gated:
                    dve.sem_inc(h_ready, 2)

                def ahead(u):
                    dve.wait_ge(transposed, u.at(1, 1))
                    for t in range(UNIT):
                        normalize(core, u, xhat[:, t], core.rstd, xhat_ready if t == UNIT - 1 else None, UNIT, t)

                def routing(u):
                    n = [0]

                    def link(ins):
                        n[0] += 1
                        ins.then_inc(route, 1)
                        dve.wait_ge(route, u.at(CHAIN, n[0]))

                    logits = small[:, 0:UNIT * EXPERTS].rearrange("p (t e) -> p t e", t=UNIT)
                    wide = lambda v: v.unsqueeze(2).to_broadcast([P, UNIT, EXPERTS])
                    dve.wait_ge(logits_made, u.at(1, 1))
                    link(nc.vector.tensor_copy(score[:], logits))
                    dve.sem_inc(settled, 1)
                    for t in range(UNIT):
                        ins = nc.vector.max(best[:, t], score[:, t])
                    link(ins)
                    dve.sem_inc(settled, 1)
                    for t in range(UNIT):
                        ins = nc.vector.max_index(index[:, t], best[:, t], score[:, t])
                    link(ins)
                    link(nc.vector.tensor_copy(index_f[:], index[:, :, 0:2]))
                    link(nc.vector.tensor_tensor(
                        one_hot[:], w["numbers"][:].unsqueeze(1).unsqueeze(1).to_broadcast([P, UNIT, 2, EXPERTS]),
                        index_f[:].unsqueeze(3).to_broadcast([P, UNIT, 2, EXPERTS]), ALU.is_equal))
                    link(nc.vector.tensor_tensor(row[:], best[:, :, 1], best[:, :, 0], ALU.subtract))
                    dve.wait_ge(squashed, u.at(1, 1))
                    link(nc.vector.tensor_scalar(pair_weight[:, :, 0], row_inv[:], -0.5, 0.5, ALU.mult, ALU.add))
                    link(nc.vector.tensor_scalar(pair_weight[:, :, 1], row_inv[:], 0.5, 0.5, ALU.mult, ALU.add))
                    link(nc.vector.tensor_tensor(chosen[:], one_hot[:, :, 0], wide(pair_weight[:, :, 0]), ALU.mult))
                    link(nc.vector.tensor_tensor(score[:], one_hot[:, :, 1], wide(pair_weight[:, :, 1]), ALU.mult))
                    link(nc.vector.tensor_tensor(weight[:], chosen[:], score[:], ALU.add))
                    assert n[0] == CHAIN
                    if biased:
                        dve.wait_ge(weighted_t, u.at(1, 1))
                        nc.vector.tensor_copy(weight_t[:], small[0:EXPERTS, :]).then_inc(wt_taken, 1)
                        dve.wait_ge(bias_made, u.at(1, 1))
                        nc.vector.tensor_tensor(unit_of(core.x, u), small[:], unit_of(core.x, u), ALU.add).then_inc(wt_taken, 1)
                        dve.wait_ge(wt_taken, u.at(2, 2))

                def half_gated(u, e, f):
                    dve.wait_ge(gated_ready, u.at(steps, 2 * e + f + 3))
                    dve.wait_ge(up_made, u.at(steps, 2 * e + f + 1))
                    nc.vector.tensor_tensor(hidden[e % 2][:, f], core.bank[2 + f][:], gate[f][:], ALU.mult).then_inc(h_ready, 1)

                def add(u, e):
                    dve.wait_ge(y_made, u.at(n_exp, e + 1))
                    if e or not biased:
                        dve.wait_ge(y_taken, u.at(n_exp, e + 2))
                    for t in range(UNIT):
                        x_u = tile_of(core.x, u, UNIT, t)
                        y = y_banks[e % 2][:, t * P:t * P + P]
                        if gated and e == 0:
                            ins = nc.vector.tensor_tensor(x_u, y, x_u, ALU.add)
                        else:
                            k = e - gated
                            ins = nc.vector.scalar_tensor_tensor(x_u, y, weight[:, t, k:k + 1], x_u, ALU.mult, ALU.add)
                    ins.then_inc(y_taken, 1)

                def body(u, then):
                    if gated:
                        for e in range(n_exp):
                            for f in range(nf):
                                half_gated(u, e, f)
                            if e == 1:
                                routing(u)
                            if e >= 1:
                                add(u, e - 1)
                            if e == 5:
                                then()
                        add(u, n_exp - 1)
                    else:
                        routing(u)
                        for e in range(n_exp):
                            add(u, e)
                            if e == 4:
                                then()
                    dve.wait_ge(y_taken, u.at(n_exp, n_exp + 2))
                    dve.wait_ge(y_taken, 1)
                    for t in range(UNIT):
                        nc.vector.bn_stats(tile_of(core.stats, u, UNIT, t), tile_of(core.x, u, UNIT, t))
                units_ahead(dve, ahead, body)

            @block.scalar
            def _(act):
                arrived(core, act, name)
                if gated:
                    act.sem_inc(gated_ready, 2)
                else:
                    act.sem_inc(hid_taken, RING)

                def take(u, j, out, func, bias):
                    act.wait_ge(hid_made, u.at(uses, j + 1))
                    nc.scalar.activation(out, core.bank[j % RING][:], func, bias=bias).then_inc(hid_taken, 1)

                def body(u):
                    act.wait_ge(transposed, u.at(1, 2))
                    nc.scalar.copy(x_t[:], t_bank[:]).then_inc(xt_taken, 1)
                    act.wait_ge(lt_made, u.at(1, 1))
                    if name == "moe2":
                        nc.scalar.copy(logits_t[:], t_bank[0:EXPERTS, :]).then_inc(lt_taken, 1)
                    else:
                        nc.scalar.activation(logits_t[:], t_bank[0:EXPERTS, :], ACT.Identity, bias=w[name + "_rb"][:, 0:1]
                                             ).then_inc(lt_taken, 1)
                    for e in range(n_exp):
                        for f in range(nf):
                            if gated:
                                act.wait_ge(gate_made, u.at(steps, 2 * e + f + 1))
                                act.wait_ge(h_ready, u.at(steps, 2 * e + f + 1))
                                nc.scalar.activation(gate[f][:], core.bank[f][:], act_fn).then_inc(gated_ready, 1)
                            else:
                                take(u, e * nf + f, hidden[e % 2][:, f], act_fn,
                                     w[name + "_b1"][:, e * nf + f:e * nf + f + 1])
                        if e == 1:
                            act.wait_ge(route, u.at(CHAIN, 6))
                            nc.scalar.activation(row_inv[:], row[:], ACT.Tanh, scale=0.5).then_inc(squashed, 1)
                units(act, body)

            @block.tensor
            def _(pe):
                arrived(core, pe, "ctx", name, "moe_const")
                pe.sem_inc(transposed, 1)

                def ring(u, j, terms):
                    pe.wait_ge(hid_taken, u.at(uses, j + 1))
                    for n, (lhs, rhs) in enumerate(terms):
                        ins = nc.tensor.matmul(core.bank[j % RING][:], lhs, rhs, start=(n == 0), stop=(n == len(terms) - 1))
                    ins.then_inc(hid_made, 1)

                def hidden_layer(u, e):
                    for f in range(nf):
                        at = slice(f * P, f * P + P)
                        if gated:
                            pe.wait_ge(gated_ready, u.at(steps, 2 * e + f + 1))
                            nc.tensor.matmul(core.bank[f][:], w["moe3_w1"][:, e, at], x_t[:], start=True, stop=True
                                             ).then_inc(gate_made, 1)
                            pe.wait_ge(h_ready, u.at(steps, 2 * e + f + 1))
                            nc.tensor.matmul(core.bank[2 + f][:], w["moe3_w3"][:, e, at], x_t[:], start=True, stop=True
                                             ).then_inc(up_made, 1)
                        else:
                            ring(u, e * nf + f, [(w[name + "_w1"][:, e, at], x_t[:])])

                def output(u, e):
                    pe.wait_ge(y_taken, u.at(n_exp, e + 1))
                    if gated:
                        pe.wait_ge(h_ready, u.at(steps, 2 * e + 4))
                    else:
                        pe.wait_ge(hid_taken, u.at(uses, (e + 1) * nf + RING))
                    for t in range(UNIT):
                        for f in range(nf):
                            ins = nc.tensor.matmul(y_banks[e % 2][:, t * P:t * P + P], hidden[e % 2][:, f, t * P:t * P + P],
                                                   w[name + "_w2"][:, e, f], start=(f == 0), stop=(f == nf - 1))
                    ins.then_inc(y_made, 1)

                def route_logits(u):
                    pe.wait_ge(lt_taken, u.at(1, 1))
                    pe.sem_inc(settled, 1)
                    for t in range(UNIT):
                        ins = nc.tensor.transpose(small[:, t * EXPERTS:(t + 1) * EXPERTS], logits_t[:, t * P:t * P + P],
                                                  w["ident"][0:EXPERTS, 0:EXPERTS])
                    ins.then_inc(logits_made, 1)

                def route_weights(u):
                    pe.wait_ge(route, u.at(CHAIN, CHAIN))
                    for t in range(UNIT):
                        ins = nc.tensor.transpose(small[0:EXPERTS, t * P:t * P + P], weight[:, t], w["ident"][:])
                    ins.then_inc(weighted_t, 1)

                def route_bias(u):
                    pe.wait_ge(wt_taken, u.at(2, 1))
                    for t in range(UNIT):
                        ins = nc.tensor.matmul(small[:, t * P:t * P + P], weight_t[:, t * P:t * P + P], w[name + "_b2"][:],
                                               start=True, stop=True)
                    ins.then_inc(bias_made, 1)

                def body(u):
                    pe.wait_ge(xhat_ready, u.at(1, 1))
                    for t in range(UNIT):
                        ins = nc.tensor.transpose(t_bank[:, t * P:t * P + P], xhat[:, t], w["ident"][:])
                    ins.then_inc(transposed, 1)
                    pe.wait_ge(xt_taken, u.at(1, 1))
                    nc.tensor.matmul(t_bank[0:EXPERTS, :], w[name + "_rw"][:], x_t[:], start=True, stop=True
                                     ).then_inc(lt_made, 1)
                    for e in range(n_exp + 1):
                        if e < n_exp:
                            hidden_layer(u, e)
                        if e >= 1:
                            output(u, e - 1)
                        if e == 0:
                            route_logits(u)
                        if e == 2 and biased:
                            route_weights(u)
                            route_bias(u)
                units(pe, body)


class RingUses:

    def __init__(self, s):
        now, before = s.inside(UNITS), s.minus(1).inside(UNITS)
        self.names = []
        for name, n, there in (("router1", 4, now), ("weights", 2, before), ("router2", 4, now),
                               ("expert", EXPERTS, before), ("output", 1, before), ("dispatch", 2, now),
                               ("output", 1, before)):
            if there:
                start = sum(name == other for other, _ in self.names)
                self.names += [(name, start + k) for k in range(n)]
        self.s = s

    def position(self, name, k):
        return self.names.index((name, k))

    def number(self, name, k, c):
        at = self.position(name, k)
        return at + c if self.s.i is None and self.s.off == 0 else self.s.at(22, at - 12 + c)

    def bank(self, name, k):
        start = 0 if self.s.i is None and self.s.off == 0 else 22 * self.s.parity - 12
        return (start + self.position(name, k)) % RING


SLOTS = 2 * CAPACITY
COLS = 96


def capacity_experts(core):
    nc, w = core.nc, core.w
    nf = 4
    half_e = EXPERTS // 2
    half = half_e * SLOTS
    assert UNIT * SLOTS <= COLS
    with ExitStack() as stack:
        sb = lambda n, shape, dt=F32: core.sb(f"moe0_{n}", shape, dt, stack)
        sem = lambda n: core.stage_sem(f"moe0_{n}")
        xhat = [sb(f"xhat{n}", [P, UNIT, P]) for n in range(2)]
        x_t = sb("x_t", [P, UTOK])
        router1, router2 = sb("router1", [P, nf, UTOK]), sb("router2", [P, nf, UTOK])
        logits_t = sb("logits_t", [EXPERTS, UTOK])
        score = sb("score", [P, UNIT, EXPERTS])
        best = sb("best", [P, UNIT, 8])
        index = sb("index", [P, UNIT, 8], U32)
        index_f = sb("index_f", [P, UNIT, 2])
        one_hot = sb("one_hot", [P, UNIT, 2, EXPERTS])
        chosen = sb("chosen", [P, UNIT, EXPERTS])
        key = sb("key", [P, UNIT * EXPERTS])
        row, row_inv = sb("row", [P, UNIT]), sb("row_inv", [P, UNIT])
        sel = sb("sel", [P, UNIT, EXPERTS, SLOTS])
        sel_w = sb("sel_w", [P, UNIT, EXPERTS, SLOTS])
        slots_x = sb("slots_x", [P, EXPERTS, COLS])
        hidden = [sb(f"hidden{n}", [P, nf, COLS]) for n in range(2)]
        slots_y = sb("slots_y", [P, UNIT, EXPERTS, SLOTS])
        y_rows = [sb(f"y_rows{g}", [P, UTOK]) for g in range(2)]
        w_rows = [sb(f"w_rows{g}", [P, UTOK]) for g in range(2)]

        zeroed = sem("zeroed")
        xhat_ready, transposed, xt_taken = sem("xhat_ready"), sem("transposed"), sem("xt_taken")
        ring_made, ring_taken = sem("ring_made"), sem("ring_taken")
        lt_made, lt_taken, logits_made = sem("lt_made"), sem("lt_taken"), sem("logits_made")
        route, squashed, placed = sem("route"), sem("squashed"), sem("placed")
        outs_made, outs_taken = sem("outs_made"), sem("outs_taken")
        y_made, added = sem("y_made"), sem("added")
        settled, settled_pe = sem("settled"), sem("settled_pe")

        t_bank, small, out_banks = core.bank[6], core.bank[7], core.bank[4:6]
        CHAIN = 14
        KEPT, KEYED, SELECTED = 11, 12, 13

        with nc.Block() as block:

            @block.sync
            def _(sp):
                start_loads(core, sp, ["moe2", "moe3"])

            @block.gpsimd
            def _(pool):
                nc.gpsimd.memset(slots_x[:], 0.0)
                for g in range(2):
                    nc.gpsimd.memset(y_rows[g][:], 0.0)
                    ins = nc.gpsimd.memset(w_rows[g][:], 0.0)
                ins.then_inc(zeroed, 1)

            @block.vector
            def _(dve):
                arrived(core, dve, "ctx", "moe0", "moe_const")

                def routing(u, first, last):
                    n = [first]

                    def link(ins):
                        n[0] += 1
                        ins.then_inc(route, 1)
                        dve.wait_ge(route, u.at(CHAIN, n[0]))

                    logits = small[:, 0:UNIT * EXPERTS].rearrange("p (t e) -> p t e", t=UNIT)
                    wide = lambda v: v.unsqueeze(2).to_broadcast([P, UNIT, EXPERTS])
                    slots = [P, UNIT * EXPERTS, SLOTS]
                    if first == 0:
                        dve.wait_ge(logits_made, u.at(1, 1))
                        link(nc.vector.tensor_reduce(row[:], logits, AX, ALU.max))
                        link(nc.vector.tensor_tensor(score[:], logits, wide(row[:]), ALU.subtract))
                        dve.wait_ge(squashed, u.at(1, 1))
                        link(nc.vector.tensor_reduce(row[:], score[:], AX, ALU.add))
                        link(nc.vector.reciprocal(row_inv[:], row[:]))
                        link(nc.vector.tensor_tensor(score[:], score[:], wide(row_inv[:]), ALU.mult))
                        dve.sem_inc(settled, 1)
                        for t in range(UNIT):
                            ins = nc.vector.max(best[:, t], score[:, t])
                        link(ins)
                        dve.sem_inc(settled, 1)
                        for t in range(UNIT):
                            ins = nc.vector.max_index(index[:, t], best[:, t], score[:, t])
                        link(ins)
                        link(nc.vector.tensor_copy(index_f[:], index[:, :, 0:2]))
                        link(nc.vector.tensor_tensor(
                            one_hot[:], w["numbers"][:].unsqueeze(1).unsqueeze(1).to_broadcast([P, UNIT, 2, EXPERTS]),
                            index_f[:].unsqueeze(3).to_broadcast([P, UNIT, 2, EXPERTS]), ALU.is_equal))
                        link(nc.vector.tensor_tensor(chosen[:], one_hot[:, :, 0], one_hot[:, :, 1], ALU.add))
                    else:
                        flat = "p t e -> p (t e)"
                        dve.wait_ge(placed, u.at(1, 1))
                        places = small[:, 0:UNIT * EXPERTS]
                        link(nc.vector.scalar_tensor_tensor(
                            chosen[:].rearrange(flat), places, float(CAPACITY), chosen[:].rearrange(flat),
                            ALU.is_lt, ALU.mult))
                        link(nc.vector.scalar_tensor_tensor(key[:], chosen[:].rearrange(flat), -64.0, places,
                                                            ALU.mult, ALU.add))
                        link(nc.vector.tensor_tensor(
                            sel[:].rearrange("p t e s -> p (t e) s"), w["slot_key"][:].unsqueeze(1).to_broadcast(slots),
                            key[:].unsqueeze(2).to_broadcast(slots), ALU.is_equal))
                        link(nc.vector.tensor_tensor(
                            sel_w[:].rearrange("p t e s -> p (t e) s"), sel[:].rearrange("p t e s -> p (t e) s"),
                            score[:].rearrange(flat).unsqueeze(2).to_broadcast(slots), ALU.mult))
                    assert n[0] == last

                def outputs(u, g):
                    dve.wait_ge(outs_made, u.at(2, 1 + g))
                    experts_g = slice(half_e * g, half_e * g + half_e)
                    outs = out_banks[g][:, 0:half_e * COLS].rearrange("p (e s) -> p e s", e=half_e)
                    nc.vector.tensor_tensor(
                        slots_y[:, :, experts_g].rearrange("p t e s -> p e t s"),
                        outs[:, :, 0:UNIT * SLOTS].rearrange("p e (t s) -> p e t s", t=UNIT),
                        w["moe0_b2"][:, experts_g].unsqueeze(2).unsqueeze(2).to_broadcast([P, half_e, UNIT, SLOTS]),
                        ALU.add).then_inc(outs_taken, 1)

                def body(s):
                    if s.inside(UNITS):
                        for t in range(UNIT):
                            normalize(core, s, xhat[s.parity][:, t], core.rstd, xhat_ready if t == UNIT - 1 else None, UNIT, t)
                    u = s.minus(2)
                    if u.inside(UNITS):
                        dve.wait_ge(y_made, u.at(1, 1))
                        nc.vector.tensor_tensor(unit_of(core.x, u), small[:], unit_of(core.x, u), ALU.add).then_inc(added, 1)
                        unit_stats(core, dve, added, u)
                    u = s.minus(1)
                    if s.inside(UNITS):
                        routing(s, 0, 10)
                    if u.inside(UNITS):
                        outputs(u, 0)
                    if s.inside(UNITS):
                        routing(s, 10, CHAIN)
                    if u.inside(UNITS):
                        outputs(u, 1)
                pipelined(dve, UNITS, 2, body)

            @block.scalar
            def _(act):
                arrived(core, act, "moe0")
                act.wait_ge(zeroed, 1)
                act.sem_inc(ring_taken, RING)

                def body(s):
                    uses = RingUses(s)

                    def bank_of(name, k):
                        act.wait_ge(ring_made, uses.number(name, k, 1))
                        return core.bank[uses.bank(name, k)]

                    def expert(e):
                        bank = bank_of("expert", e)
                        for f in range(nf):
                            ins = nc.scalar.activation(hidden[e % 2][:, f], bank[:, f * COLS:(f + 1) * COLS], ACT.Relu,
                                                       bias=w["moe0_b1"][:, e * nf + f:e * nf + f + 1])
                        ins.then_inc(ring_taken, 1)

                    def rows(name, g, out):
                        bank = bank_of(name, g)
                        nc.scalar.copy(out[g][0:half, :], bank[0:half, :]).then_inc(ring_taken, 1)

                    now, before = s.inside(UNITS), s.minus(1).inside(UNITS)
                    if now:
                        act.wait_ge(transposed, s.at(1, 1))
                        nc.scalar.copy(x_t[:], t_bank[:]).then_inc(xt_taken, 1)
                        for f in range(nf):
                            bank = bank_of("router1", f)
                            nc.scalar.activation(router1[:, f], bank[:], ACT.Relu, bias=w["moe0_rb1"][:, f:f + 1]
                                                 ).then_inc(ring_taken, 1)
                    if before:
                        for g in range(2):
                            rows("weights", g, w_rows)
                    if now:
                        for f in range(nf):
                            bank = bank_of("router2", f)
                            nc.scalar.activation(router2[:, f], bank[:], ACT.Relu, bias=w["moe0_rb2"][:, f:f + 1]
                                                 ).then_inc(ring_taken, 1)
                    if before:
                        expert(0)
                    if now:
                        act.wait_ge(lt_made, s.at(1, 1))
                        nc.scalar.activation(logits_t[:], t_bank[0:EXPERTS, :], ACT.Identity, bias=w["moe0_rb"][:, 0:1]
                                             ).then_inc(lt_taken, 1)
                    if before:
                        for e in range(1, 3):
                            expert(e)
                    if now:
                        act.wait_ge(route, s.at(CHAIN, 2))
                        nc.scalar.activation(score[:], score[:], ACT.Exp).then_inc(squashed, 1)
                    if before:
                        for e in range(3, EXPERTS):
                            expert(e)
                        rows("output", 0, y_rows)
                    if now:
                        for d in range(2):
                            bank = bank_of("dispatch", d)
                            nc.scalar.copy(
                                slots_x[:, :, 2 * d * SLOTS:2 * (d + 1) * SLOTS].rearrange("p e (t s) -> p e t s", t=2),
                                bank[:, 0:2 * EXPERTS * SLOTS].rearrange("p (t e s) -> p e t s", t=2, e=EXPERTS)
                            ).then_inc(ring_taken, 1)
                    if before:
                        rows("output", 1, y_rows)
                pipelined(act, UNITS, 1, body)

            @block.tensor
            def _(pe):
                arrived(core, pe, "ctx", "moe0", "moe_const")
                pe.wait_ge(zeroed, 1)

                def body(s):
                    uses = RingUses(s)
                    u = s.minus(1)
                    now, before = s.inside(UNITS), u.inside(UNITS)

                    def bank_of(name, k):
                        pe.wait_ge(ring_taken, uses.number(name, k, 1))
                        return core.bank[uses.bank(name, k)]

                    def wait_taken(name, k):
                        pe.wait_ge(ring_taken, uses.number(name, k, 1 + RING))

                    def total(out, terms, done):
                        for n, (lhs, rhs) in enumerate(terms):
                            ins = nc.tensor.matmul(out, lhs, rhs, start=(n == 0), stop=(n == len(terms) - 1))
                        if done is not None:
                            ins.then_inc(done, 1)

                    def hidden_layer(e):
                        bank = bank_of("expert", e)
                        for f in range(nf):
                            total(bank[:, f * COLS:(f + 1) * COLS],
                                  [(w["moe0_w1"][:, e, f * P:f * P + P], slots_x[:, e])], ring_made if f == nf - 1 else None)

                    def output(e):
                        wait_taken("expert", e)
                        if e % half_e == 0 and u.past(1):
                            pe.wait_ge(outs_taken, u.at(2, -1 + e // half_e))
                        at = slice(e % half_e * COLS, (e % half_e + 1) * COLS)
                        total(out_banks[e // half_e][:, at], [(w["moe0_w2"][:, e, f], hidden[e % 2][:, f]) for f in range(nf)],
                              outs_made if e % half_e == half_e - 1 else None)

                    def rows(name, g, source):
                        bank = bank_of(name, g)
                        for t in range(UNIT):
                            ins = nc.tensor.transpose(
                                bank[0:half, t * P:t * P + P],
                                source[:, t, half_e * g:half_e * g + half_e].rearrange("p e s -> p (e s)"), w["ident"][:])
                        ins.then_inc(ring_made, 1)

                    if now:
                        pe.wait_ge(xhat_ready, s.at(1, 1))
                        for t in range(UNIT):
                            ins = nc.tensor.transpose(t_bank[:, t * P:t * P + P], xhat[s.parity][:, t], w["ident"][:])
                        ins.then_inc(transposed, 1)
                        pe.wait_ge(xt_taken, s.at(1, 1))
                        for f in range(nf):
                            total(bank_of("router1", f)[:], [(w["moe0_rw1"][:, f * P:f * P + P], x_t[:])], ring_made)
                    if before:
                        pe.wait_ge(route, u.at(CHAIN, CHAIN))
                        for g in range(2):
                            rows("weights", g, sel_w)
                    if now:
                        wait_taken("router1", nf - 1)
                        for g in range(nf):
                            total(bank_of("router2", g)[:],
                                  [(w["moe0_rw2"][:, f, g * P:g * P + P], router1[:, f]) for f in range(nf)], ring_made)
                    if before:
                        wait_taken("weights", 1)
                        hidden_layer(0)
                    if now:
                        wait_taken("router2", nf - 1)
                        total(t_bank[0:EXPERTS, :], [(w["moe0_rw"][:, f], router2[:, f]) for f in range(nf)], lt_made)
                    for e in range(1, EXPERTS + 1):
                        if before:
                            if e < EXPERTS:
                                hidden_layer(e)
                            output(e - 1)
                        if now and e == 1:
                            pe.wait_ge(lt_taken, s.at(1, 1))
                            if s.past(2):
                                pe.wait_ge(added, s.at(1, -1))
                            pe.sem_inc(settled_pe, 1)
                            for t in range(UNIT):
                                ins = nc.tensor.transpose(small[:, t * EXPERTS:(t + 1) * EXPERTS], logits_t[:, t * P:t * P + P],
                                                          w["ident"][0:EXPERTS, 0:EXPERTS])
                            ins.then_inc(logits_made, 1)
                        if now and e == 6:
                            pe.wait_ge(route, s.at(CHAIN, 10))
                            total(small[:, 0:UNIT * EXPERTS], [(w["earlier"][:], chosen[:].rearrange("p t e -> p (t e)"))], placed)
                    if before:
                        pe.wait_ge(outs_taken, u.at(2, 1))
                        rows("output", 0, slots_y)
                    if now:
                        pe.wait_ge(route, s.at(CHAIN, SELECTED))
                        for d in range(2):
                            bank = bank_of("dispatch", d)
                            for k in range(2):
                                t = 2 * d + k
                                ins = nc.tensor.matmul(bank[:, k * EXPERTS * SLOTS:(k + 1) * EXPERTS * SLOTS], xhat[s.parity][:, t],
                                                       sel[:, t].rearrange("p e s -> p (e s)"), start=True, stop=True)
                            ins.then_inc(ring_made, 1)
                    if before:
                        pe.wait_ge(outs_taken, u.at(2, 2))
                        rows("output", 1, slots_y)
                        wait_taken("output", 1)
                        for t in range(UNIT):
                            at = slice(t * P, t * P + P)
                            total(small[:, at], [(w_rows[g][:, at], y_rows[g][:, at]) for g in range(2)],
                                  y_made if t == UNIT - 1 else None)
                pipelined(pe, UNITS, 1, body)


def by_query(mask):
    rows = mask.reshape(TILES, 2, 1, SEQ).transpose(1, 2, 0, 3)
    return np.broadcast_to(rows, (2, SEQ, TILES, SEQ)).reshape(P, TILES, SEQ)


def twice_rows(weights):
    rows = weights.reshape(2, 4, 1, 16, -1).transpose(1, 2, 3, 0, 4)
    return np.broadcast_to(rows, (4, 2, 16, 2, rows.shape[-1])).reshape(P, 2, -1)


def by_group(weights):
    return weights.reshape(-1, P, weights.shape[-1]).transpose(1, 0, 2)


def outputs_of(weights):
    return weights.reshape(weights.shape[0], -1, P, weights.shape[-1]).transpose(2, 0, 1, 3)


def store(core, out):
    stored = core.sem("stored")
    with core.nc.Block() as block:

        @block.sync
        def _(sp):
            half = TILES // 2
            for q in range(2):
                sp.dma_start(out.rearrange("(t p) c -> p t c", p=P)[:, q * half:(q + 1) * half, :],
                             core.x[:, q * half:(q + 1) * half, :]).then_inc(stored, DMA_INC)
            sp.wait_ge(stored, 2 * DMA_INC)


def program(nc, args, out):
    with ExitStack() as stack:
        core = Core(nc, stack, args)
        resident = ["ctx", "const", "attn1", "moe0", "moe_const", "fp8", "attn2", "attn3"]
        allocate(core, resident)
        core.w["minus_huge"] = core.sb("minus_huge", [2, TILES, SEQ], BF16)
        core.w["batch_rows_bf"] = core.sb("batch_rows_bf", [2, P], BF16)
        with ExitStack() as early:
            allocate(core, ["wide", "mask_i"], early)
            load_and_first_stats(core, ["ctx", "wide"] + resident[1:] + ["mask_i"])
            norm_scale(core, 0)
            wide_attention(core)
            core.end_of_stage()
            prepare_mask(core)
        allocate(core, ["moe2", "moe3"])
        norm_scale(core, 1)
        capacity_experts(core)
        core.end_of_stage()
        norm_scale(core, 2)
        narrow_attention(core, "attn1", True, True)
        core.end_of_stage()
        norm_scale(core, 3)
        fp8_product(core)
        core.end_of_stage()
        norm_scale(core, 4)
        narrow_attention(core, "attn2", False, False)
        core.end_of_stage()
        norm_scale(core, 5)
        experts(core, "moe2")
        core.end_of_stage()
        norm_scale(core, 6)
        narrow_attention(core, "attn3", True, False)
        core.end_of_stage()
        norm_scale(core, 7)
        experts(core, "moe3")
        store(core, out)


def kernel(**inputs):
    import concourse.bacc as bacc
    from concourse.bass_utils import run_bass_kernel_spmd

    a = {name: np.asarray(value) for name, value in inputs.items()}
    laid = {}
    laid["x"] = a["x"].reshape(TOKENS, D)
    laid["ident"] = np.eye(P, dtype=np.float32)
    laid["ctx_t"] = a["ctx_1024"].reshape(TILES, P, D).transpose(2, 0, 1)
    mask_f = a["mask_BxS2_fk1"]
    laid["mask_f_rows"] = mask_f.reshape(TILES, P)
    laid["mask_f_col"] = mask_f.reshape(TILES, P).T
    laid["mask_f_keys"] = by_query(mask_f)
    laid["wide_wq"], laid["wide_wk"], laid["wide_wv"] = a["L0_xattn_Wq"], a["L0_xattn_Wk"], a["L0_xattn_Wv"]
    laid["wide_wo"] = a["L0_xattn_Wo"].reshape(8, P, D).transpose(1, 0, 2)

    heads, halves, batches = np.arange(P) // 8, np.arange(P) // SEQ, np.arange(P) // 16 % 2
    pair_half = np.arange(P) // 8 % 2
    laid["head_mask"] = (heads[:, None] == np.arange(HEADS)).astype(np.float32)
    laid["batch_mask"] = (batches[:, None] == np.arange(2)).astype(np.float32)
    laid["block_mask"] = ((2 * pair_half + batches)[:, None] == np.arange(4)).astype(np.float32)
    laid["half_ones"] = (halves[:, None] == pair_half[:32]).astype(np.float32)
    laid["mask_i_rows"] = a["mask_BxS2_ik0"].reshape(TILES, 2, SEQ).transpose(1, 0, 2)
    laid["batch_rows"] = (np.arange(2)[:, None] == halves).astype(np.float32)
    for n, (wq, wk, wv, wo) in {
        1: (a["L1_xattn_q_w"].T, a["L1_xattn_k_w"].T, a["L1_xattn_v_w"].T, np.eye(P, dtype=np.float32)),
        2: (a["L2_xattn_Wq"], a["L2_xattn_Wk"], a["L2_xattn_Wv"], a["L2_xattn_Wo"]),
        3: (a["L3_xattn_q_w"].T, a["L3_xattn_k_w"].T, a["L3_xattn_v_w"].T, a["L3_xattn_o_w"].T),
    }.items():
        laid[f"attn{n}_wq"], laid[f"attn{n}_wk"], laid[f"attn{n}_wv"] = wq, wk, wv
        laid[f"attn{n}_wo"] = twice_rows(wo)
    column = lambda v: v.reshape(-1, P).T
    row = lambda v: np.broadcast_to(v[None, :], (P, v.shape[0]))
    laid["attn1_bq"], laid["attn1_bk"] = column(a["L1_xattn_q_b"]), column(a["L1_xattn_k_b"])
    laid["attn1_bo"] = row(a["L1_xattn_v_b"])
    laid["attn2_bq"], laid["attn2_bk"] = column(a["L2_xattn_bq"]), column(a["L2_xattn_bk"])
    laid["attn2_bv"], laid["attn2_bo"] = row(a["L2_xattn_bv"]), row(a["L2_xattn_bo"])
    laid["attn3_bq"], laid["attn3_bk"] = column(a["L3_xattn_q_b"]), column(a["L3_xattn_k_b"])
    laid["attn3_bv"] = row(a["L3_xattn_v_b"]).T
    laid["attn3_bo"] = row(a["L3_xattn_o_b"])
    laid["attn3_wo_plain"] = a["L3_xattn_o_w"].T

    laid["numbers"] = np.broadcast_to(np.arange(EXPERTS, dtype=np.float32), (P, EXPERTS))
    token = np.arange(P)
    earlier = (token[:, None] // SEQ == token[None, :] // SEQ) & (token[:, None] < token[None, :])
    laid["earlier"] = earlier.astype(np.float32)
    slots = np.arange(2 * CAPACITY) - 64
    laid["slot_key"] = (slots[None, :] - CAPACITY * halves[:, None]).astype(np.float32)
    laid["moe0_rw1"], laid["moe0_rb1"] = a["L0_ffn_rW1"], column(a["L0_ffn_rb1"])
    laid["moe0_rw2"], laid["moe0_rb2"] = by_group(a["L0_ffn_rW2"]), column(a["L0_ffn_rb2"])
    laid["moe0_rw"], laid["moe0_rb"] = by_group(a["L0_ffn_rW3"]), a["L0_ffn_rb3"][:, None]
    laid["moe0_w1"], laid["moe0_b1"] = a["L0_ffn_eW1"].transpose(1, 0, 2), column(a["L0_ffn_eb1"])
    laid["moe0_w2"], laid["moe0_b2"] = outputs_of(a["L0_ffn_eW2"]), a["L0_ffn_eb2"].T
    laid["moe2_rw"] = a["L2_ffn_router_w"].T
    laid["moe2_w1"], laid["moe2_b1"] = a["L2_ffn_w1"].transpose(2, 0, 1), column(a["L2_ffn_b1"])
    laid["moe2_w2"], laid["moe2_b2"] = outputs_of(a["L2_ffn_w2"].transpose(0, 2, 1)), a["L2_ffn_b2"]
    laid["moe3_rw"], laid["moe3_rb"] = a["L3_ffn_router_w"].T, a["L3_ffn_experts_bias"][:, None]
    with_shared = lambda shared, own: np.concatenate([a["L3_ffn_" + shared], a["L3_ffn_" + own]])
    laid["moe3_w1"] = with_shared("sw1", "w1").transpose(1, 0, 2)
    laid["moe3_w3"] = with_shared("sw3", "w3").transpose(1, 0, 2)
    laid["moe3_w2"] = outputs_of(with_shared("sw2", "w2"))
    laid["fp8_kernel"] = a["L1_ffn_kernel"]
    laid["fp8_scales"] = row(np.concatenate([a["L1_ffn_input_scale"], a["L1_ffn_kernel_scale"]]))
    laid["fp8_bias"] = row(a["L1_ffn_bias"])


    nc = bacc.Bacc("TRN2", target_bir_lowering=False, num_devices=1)
    arrays, args = {}, {}
    for name, value in laid.items():
        value = np.ascontiguousarray(value)
        arrays["in_" + name] = value
        args[name] = nc.dram_tensor("in_" + name, value.shape, mybir.dt.from_np(value.dtype), kind="ExternalInput").ap()
    out = nc.dram_tensor("out", (TOKENS, D), F32, kind="ExternalOutput").ap()
    program(nc, args, out)
    result = run_bass_kernel_spmd(nc, [arrays], core_ids=[0])
    return result.results[0]["out"].reshape(64, SEQ, D)
```
